# Optimizing a Trainium2 kernel written in Bass

```python
import numpy as np
import jax
import jax.numpy as jnp

def _softmax(x, axis=-1):
    return jax.nn.softmax(x, axis=axis)

def _gelu(x):
    return jax.nn.gelu(x, approximate=True)

def _silu(x):
    return jax.nn.silu(x)

def _sigmoid(x):
    return jax.nn.sigmoid(x)

def _layernorm(x, axis=-1, eps=1e-05):
    m = jnp.mean(x, axis=axis, keepdims=True)
    v = jnp.var(x, axis=axis, keepdims=True)
    return (x - m) / jnp.sqrt(v + eps)

def _scatter_add(tgt, idx, src, axis=0):
    return tgt.at[idx].add(src)

def _segment_sum(src, seg, n):
    return jax.ops.segment_sum(src, seg, n)
kernel_name = 'mk_adj_ffn_d1_adj_r2_445327'

def setup_inputs(seed: int=0):
    np.random.seed(seed)
    _w = jnp.asarray

    def _rec_inputs():
        import jax
        import jax.numpy as jnp
        _gk = jax.random.key(seed)
        x = -0.0002928 + 1 * jax.random.normal(jax.random.fold_in(_gk, 1), (4096, 256), jnp.float32)
        _a = jax.random.bernoulli(jax.random.fold_in(_gk, 2), 0.00390625, (4096, 4096))
        _a = jnp.logical_or(_a, jnp.swapaxes(_a, -1, -2))
        _a = jnp.logical_or(_a, jnp.eye(4096, dtype=bool))
        adj = _a.astype(jnp.int32)
        return (x, adj)
    x, adj = _rec_inputs()

    def _L0_gnn_setup():
        import jax, jax.numpy as jnp
        import numpy as np
        N, D_IN, D_OUT = (4096, 256, 256)
        key = jax.random.key(seed)
        ks = jax.random.split(key, 8)
        scale_in = 1.0 / np.sqrt(D_IN)
        scale_cat = 1.0 / np.sqrt(2 * D_OUT)
        return {'x': jax.random.normal(ks[0], (N, D_IN), dtype=jnp.float32), 'adj': jax.random.randint(ks[1], (N, N), 0, 2, dtype=jnp.int32), 'W_self': jax.random.uniform(ks[2], (D_IN, D_OUT), jnp.float32, -scale_in, scale_in), 'b_self': jax.random.uniform(ks[3], (D_OUT,), jnp.float32, -scale_in, scale_in), 'W_nb': jax.random.uniform(ks[4], (D_IN, D_OUT), jnp.float32, -scale_in, scale_in), 'b_nb': jax.random.uniform(ks[5], (D_OUT,), jnp.float32, -scale_in, scale_in), 'W_comb': jax.random.uniform(ks[6], (2 * D_OUT, D_OUT), jnp.float32, -scale_cat, scale_cat), 'b_comb': jax.random.uniform(ks[7], (D_OUT,), jnp.float32, -scale_cat, scale_cat)}
    _L0_gnn_all = _L0_gnn_setup()
    _L0_gnn_in = {k: v for k, v in _L0_gnn_all.items() if k in ('W_self', 'b_self', 'W_nb', 'b_nb', 'W_comb', 'b_comb')}
    del _L0_gnn_all

    def _L0_ffn_setup():
        import jax, jax.numpy as jnp
        import numpy as np
        B, T, D = (4, 1024, 256)
        E, H, K = (8, 256, 2)
        key = jax.random.key(seed)
        ks = jax.random.split(key, 8)
        s_in = 1.0 / np.sqrt(D)
        s_h = 1.0 / np.sqrt(H)
        return {'x': jax.random.normal(ks[0], (B, T, D), dtype=jnp.float32), 'Wg': jax.random.uniform(ks[1], (D, E), jnp.float32, -s_in, s_in), 'bg': jax.random.uniform(ks[2], (E,), jnp.float32, -s_in, s_in), 'W1': jax.random.uniform(ks[3], (E, D, H), jnp.float32, -s_in, s_in), 'b1': jax.random.uniform(ks[4], (E, H), jnp.float32, -s_in, s_in), 'W2': jax.random.uniform(ks[5], (E, H, H), jnp.float32, -s_h, s_h), 'b2': jax.random.uniform(ks[6], (E, H), jnp.float32, -s_h, s_h)}
    _L0_ffn_all = _L0_ffn_setup()
    _L0_ffn_in = {k: v for k, v in _L0_ffn_all.items() if k in ('Wg', 'bg', 'W1', 'b1', 'W2', 'b2')}
    del _L0_ffn_all
    return {'x': x, 'adj': adj, 'L0_gnn_W_self': _L0_gnn_in['W_self'], 'L0_gnn_b_self': _L0_gnn_in['b_self'], 'L0_gnn_W_nb': _L0_gnn_in['W_nb'], 'L0_gnn_b_nb': _L0_gnn_in['b_nb'], 'L0_gnn_W_comb': _L0_gnn_in['W_comb'], 'L0_gnn_b_comb': _L0_gnn_in['b_comb'], 'L0_ffn_Wg': _L0_ffn_in['Wg'], 'L0_ffn_bg': _L0_ffn_in['bg'], 'L0_ffn_W1': _L0_ffn_in['W1'], 'L0_ffn_b1': _L0_ffn_in['b1'], 'L0_ffn_W2': _L0_ffn_in['W2'], 'L0_ffn_b2': _L0_ffn_in['b2']}

def reference(x, adj, L0_gnn_W_self, L0_gnn_b_self, L0_gnn_W_nb, L0_gnn_b_nb, L0_gnn_W_comb, L0_gnn_b_comb, L0_ffn_Wg, L0_ffn_bg, L0_ffn_W1, L0_ffn_b1, L0_ffn_W2, L0_ffn_b2):
    import jax
    import jax.numpy as jnp

    def _L0_gnn_ref(x, adj, W_self, b_self, W_nb, b_nb, W_comb, b_comb):
        import jax, jax.numpy as jnp
        import numpy as np
        N, D_IN, D_OUT = (4096, 256, 256)
        mask = (adj > 0).astype(x.dtype)
        deg = jnp.sum(mask, axis=1, keepdims=True)
        agg = mask @ x / jnp.maximum(deg, 1.0)
        self_f = x @ W_self + b_self
        nb_f = agg @ W_nb + b_nb
        combined = jnp.concatenate([self_f, nb_f], axis=-1)
        out = combined @ W_comb + b_comb
        return jax.nn.relu(out)

    def _L0_ffn_ref(x, Wg, bg, W1, b1, W2, b2):
        import jax, jax.numpy as jnp
        import numpy as np
        B, T, D = (4, 1024, 256)
        E, H, K = (8, 256, 2)
        Bx, Tx, Dx = x.shape
        xf = x.reshape(-1, Dx)
        logits = xf @ Wg + bg
        topk_scores, topk_idx = jax.lax.top_k(logits, K)
        topk_w = jax.nn.softmax(topk_scores, axis=-1)
        h = jax.nn.gelu(jnp.einsum('nd,edh->neh', xf, W1) + b1, approximate=False)
        y = jnp.einsum('neh,ehf->nef', h, W2) + b2
        sel = jnp.take_along_axis(y, topk_idx[:, :, None], axis=1)
        out = jnp.sum(topk_w[:, :, None] * sel, axis=1)
        return out.reshape(Bx, Tx, -1)
    x = x + _L0_gnn_ref(_layernorm(x, axis=-1), adj, L0_gnn_W_self, L0_gnn_b_self, L0_gnn_W_nb, L0_gnn_b_nb, L0_gnn_W_comb, L0_gnn_b_comb)
    x = x + _L0_ffn_ref(_layernorm(x, axis=-1)[None], L0_ffn_Wg, L0_ffn_bg, L0_ffn_W1, L0_ffn_b1, L0_ffn_W2, L0_ffn_b2)[0]
    return x

_drawn_inputs = setup_inputs


def setup_inputs(seed=0):
    import zlib

    import numpy as np

    out = dict(_drawn_inputs(seed))
    spreads = {}
    factors = {'L0_gnn_b_self': 4.018, 'L0_gnn_b_nb': 3.623, 'L0_ffn_b1': 6.471}
    for name, (base, spread) in spreads.items():
        noise = np.random.default_rng([zlib.crc32(name.encode()), seed]).standard_normal(out[name].shape)
        drawn = base * np.exp(spread * noise) if base else spread * noise
        out[name] = jnp.asarray(drawn.astype(out[name].dtype))
    for name, factor in factors.items():
        out[name] = (out[name] * factor).astype(out[name].dtype)
    return out
```

```python
from contextlib import ExitStack

import concourse.bass as bass
from concourse import mybir

ALU = mybir.AluOpType
ACT = mybir.ActivationFunctionType
AX = mybir.AxisListType
F32 = mybir.dt.float32
F16 = mybir.dt.float16
F8 = mybir.dt.float8e4
I32 = mybir.dt.int32
U32 = mybir.dt.uint32
RED = bass.bass_isa.ReduceOp

P = 128
Q = 32
G = P // Q
EPS = 1e-5
XS = 2.0 ** 11


def gnn_moe_kernel(nc, x, adj, W_self, b_self, W_nb, b_nb, W_comb, b_comb, Wg, bg, W1, b1, W2, b2, out):
    N, D = x.shape
    E, _, H = W1.shape
    NT = N // P
    B = 4
    NG = NT // B
    KT = D // P
    NQ = N // G
    TT = 2 * P
    CAP = N + TT
    ET = -(-((2 * N + E * (TT - 1)) // TT) // B) * B
    DUM = ET - 2 * N // TT
    RW = 2 * D + 2
    assert D == H == 2 * P and N % (G * P) == 0 and E == 8 and B == 4

    xs_dram = nc.dram_tensor("dispatched", (E * CAP + DUM * TT, RW), F16, kind="Internal").ap()
    yp_dram = nc.dram_tensor("pair_out", (2 * N + (E + DUM) * TT, D), F32, kind="Internal").ap()

    x_v = x.rearrange("(g k c e) d -> g k c (e d)", g=G, k=NG, c=Q, e=B)
    out_v = out.rearrange("(g k c e) d -> g k c (e d)", g=G, k=NG, c=Q, e=B)
    adj_v = adj.rearrange("(b k r e) (g j) -> k e g r b j", b=G, k=NG, r=Q, e=B, g=G)
    yp_v = yp_dram[0:2 * N, :].rearrange("(g k c e) d -> g k c (e d)", g=G, k=NG, c=Q, e=2 * B)

    with ExitStack() as ctx:
        def sb(name, shape, dt):
            return ctx.enter_context(nc.sbuf_tensor(name, shape, dt))

        def sem(name):
            return ctx.enter_context(nc.semaphore(name))

        bank = [ctx.enter_context(nc.psum_tensor(f"bank{i}", [P, 512], F32)) for i in range(8)]
        acc = bank[0:2]
        hps = bank[0:2] + bank[6:8]
        zbank = bank[0:2] + bank[4:6]
        tps = bank[2:4]
        fold = bank[4:6]
        wps = bank[6:8]
        cbank = bank[7]
        lbank, rbank, tbank = bank[4:6], bank[7], bank[6]

        x_sb = sb("x_sb", [P, NT, D], F32)
        rows = sb("rows", [P, NT * RW], F16)
        row16 = rows[:, :].rearrange("p (t d) -> p t d", t=NT)
        self_sb = rows[:, :].bitcast(F32).rearrange("p (t d) -> p t d", t=NT)
        z_flat = sb("z_flat", [P, NT * (D + 1)], F16)
        z_hi = z_flat[:, :].rearrange("p (t d) -> p t d", t=NT)
        z_lo = sb("z_lo", [P, NT, D], F16)
        stage = sb("stage", [P, 4, 2, NQ], I32)
        mask = sb("mask", [P, 2, G, NQ], F8)
        maskT = sb("maskT", [P, 4, G * NQ], F8)
        w12 = sb("w12", [P, E, 2, 2, KT, H], F16)
        wst = sb("wst", [P, 2, KT, H], F32)
        b1c = sb("b1c", [P, E, KT], F32)
        wg_f = sb("wg_f", [P, KT, E], F32)
        wg_s = sb("wg_s", [P, 2, KT, E], F16)
        bg_bc = sb("bg_bc", [P, E], F32)
        bc_bc = sb("bc_bc", [P, D], F32)
        const_bc = sb("const_bc", [P, D], F32)
        bcol = sb("bcol", [P, 2, KT], F32)
        diff = sb("diff", [P, P], I32)
        ident = sb("ident", [P, P], F16)
        identf = sb("identf", [P, P], F32)
        upper = sb("upper", [P, P], F16)
        ones = sb("ones", [P, P], F16)
        iota8 = sb("iota8", [P, E], F32)
        region = sb("region", [P, E], F32)
        mhalf = sb("mhalf", [P, B], F32)
        pid = sb("pid", [P, NT, 2], I32)
        st6 = sb("st6", [P, 2, B, 6], F32)
        mv = sb("mv", [P, B, 2], F32)
        ve = sb("ve", [P, 2, NT], F32)
        rs = sb("rs", [P, 2, NT], F32)
        nbx = sb("nbx", [P, NT], F32)
        mv2 = sb("mv2", [P, B, 2], F32)
        xh = sb("xh", [P, 2, D], F32)
        xT = sb("xT", [P, 4, 4 * P], F16)
        sdeg = sb("sdeg", [P, 4], F32)
        rdeg = sb("rdeg", [P, 4], F32)
        tsum = sb("tsum", [P, 2, D], F32)
        lg = sb("lg", [P, B, E], F32)
        top = sb("top", [P, B, 8], F32)
        tidx = sb("tidx", [P, B, 8], U32)
        tidf = sb("tidf", [P, B, 2], F32)
        hot = sb("hot", [P, 2, B, E], F32)
        both = sb("both", [P, B, E], F16)
        base = sb("base", [P, B + 1, E], F16)
        m100 = sb("m100", [P, 1], F32)
        rk = sb("rk", [P, B, E], F32)
        pick = sb("pick", [P, 2, B, E], F32)
        slotf = sb("slotf", [P, 2, B], F32)
        slot = sb("slot", [P, NT, 2], I32)
        m12 = sb("m12", [P, NT, 2], F32)
        wdif = sb("wdif", [P, NT], F32)
        wexp = sb("wexp", [P, NT], F32)
        wden = sb("wden", [P, NT], F32)
        wts = sb("wts", [P, 2, NT], F32)
        fmx = sb("fmx", [P, 2], F32)
        fmr = sb("fmr", [P, 2], F32)
        fcl = sb("fcl", [P, 2], F32)
        fp2 = sb("fp2", [P, 2], F32)
        fin = sb("fin", [P, 2], F32)
        scw = sb("scw", [P, 5], F32)
        emx = sb("emx", [P, 3], F32)
        emr = sb("emr", [P, 3], F32)
        ecl = sb("ecl", [P, 3], F32)
        ep2 = sb("ep2", [P, 3], F32)
        ein = sb("ein", [P, 3], F32)
        s12 = sb("s12", [P, 2], F32)
        sc1 = sb("sc1", [P, E], F32)
        shs = sb("shs", [P, E], F32)
        sc2 = sb("sc2", [P, E], F32)
        cntt = sb("cntt", [P, E], F32)
        nti = sb("nti", [P, E], F32)
        cinc = sb("cinc", [P, E], F32)
        coef = sb("coef", [P, E], F32)
        onesE = sb("onesE", [P, E], F32)
        texp = sb("texp", [P, ET], F32)
        tjmp = sb("tjmp", [P, ET], F32)
        padf = sb("padf", [P, E], F32)
        tab = sb("tab", [P, 2, ET], I32)
        padrow = sb("padrow", [P, E], I32)
        enum = sb("enum", [P, 4, 2], I32)
        pad = sb("pad", [P, 2, 2 * D], F16)
        padn = sb("padn", [P, E + DUM, 2], I32)

        mask16 = mask[:, :, :, :].rearrange("p a b c -> p (a b c)").bitcast(F16)
        wf = mask16[:, 0:4 * KT * D].rearrange("p (q t n) -> p q t n", q=2, t=KT)
        hl = mask16[:, 4 * KT * D:4 * KT * D + 8 * D].rearrange("p (a n) -> p a n", a=4)
        b2_bc = z_flat[:, :].bitcast(F32)[:, 0:E * H].rearrange("p (e n) -> p e n", e=E)

        ring = stage[:, :, :, :].rearrange("p a b c -> p (a b c)").bitcast(F32)
        cuts = [0]

        def cut(n):
            cuts[0] += n
            assert cuts[0] <= 8 * NQ
            return ring[:, cuts[0] - n:cuts[0]]

        wraw = cut(4 * KT * D).rearrange("p (w t n) -> p w t n", w=4, t=KT)
        wT = cut(2 * KT * D).rearrange("p (w t n) -> p w t n", w=2, t=KT)
        wsum = cut(2 * KT * D).rearrange("p (t n) -> p t n", t=KT)
        bbig = cut(2 * KT * P).rearrange("p (w t n) -> p w t n", w=2, t=KT)
        cuts[0] = 0
        R = 4
        erow = cut(R * RW).bitcast(F16).rearrange("p (a s n) -> p a s n", a=R, s=2)
        ehid = cut(2 * TT * KT).rearrange("p (a t n) -> p a t n", a=2, t=KT)
        ehl = cut(2 * TT * KT).bitcast(F16).rearrange("p (a q t n) -> p a q t n", a=2, q=2, t=KT)
        exT = cut(2 * TT * KT).bitcast(F16).rearrange("p (a q n) -> p a (q n)", a=2, q=4)
        tio = cut(ET * E).rearrange("p (t e) -> p t e", t=ET)
        tge = cut(ET * E).rearrange("p (t e) -> p t e", t=ET)
        tgc = cut(ET * E).rearrange("p (t e) -> p t e", t=ET)
        q256 = cut(E * N // TT).rearrange("p (e q) -> p e q", e=E)
        cmpq = cut(E * N // TT).rearrange("p (e q) -> p e q", e=E)
        ysb = self_sb[:, 0:2 * R, 0:D].rearrange("p (a s) n -> p a s n", s=2)
        yin = z_lo[:, :, :].rearrange("p t n -> p (t n)").bitcast(F32).rearrange("p (a e k n) -> p a e k n", a=2, e=B, k=2)

        tp16 = [b_[:, 0:2 * P].bitcast(F16) for b_ in tps]
        etp16 = [b_[:, :].bitcast(F16) for b_ in tps]
        mask32 = [mask[:, i].rearrange("p b j -> p (b j)").bitcast(U32).rearrange("p (b k w) -> p b k w", b=G, k=NG) for i in range(2)]
        maskT32 = [maskT[:, i].bitcast(U32).rearrange("p (k b w) -> p b k w", b=G, k=NG) for i in range(4)]
        maskT8 = [maskT[:, i].rearrange("p (k m e) -> p k m e", k=NG, e=B) for i in range(4)]

        s_w, s_small, s_b12 = sem("weights_loaded"), sem("small_loaded"), sem("expert_biases_loaded")
        s_x = [sem("x0_loaded"), sem("x1_loaded"), sem("x2_loaded"), sem("x_rest_loaded")]
        s_iot, s_b2 = sem("table_iotas"), sem("b2_loaded")
        s_io, s_cst, s_idt, s_pad = sem("iotas"), sem("constants"), sem("identity"), sem("pad_rows")
        s_wtp, s_wtc, s_fold, s_wsum = sem("weights_transposed"), sem("wT_copied"), sem("weights_folded"), sem("fold_copied")
        s_fmx, s_fmr, s_fch, s_wf, s_bb, s_cp, s_cb = (sem(n) for n in (
            "fold_max", "fold_max_all", "fold_chain", "fold_split", "bias_spread", "const_product", "const_row"))
        s_st, s_ve, s_rs, s_nb = sem("stats_chain"), sem("variance"), sem("rstd"), sem("norm_scales")
        s_xh, s_hi, s_lo, s_tp, s_xT = sem("normalised"), sem("hi"), sem("lo"), sem("transposed"), sem("transposed_copied")
        s_zp, s_zhi, s_zlo, s_self = sem("setup_product"), sem("z_hi_made"), sem("z_lo_made"), sem("self_made")
        s_adj = [sem(f"adj_loaded{i}") for i in range(4)]
        s_mD, s_mA, s_T, s_mm = sem("mask_by_vector"), sem("mask_by_scalar"), sem("mask_transposed"), sem("neighbours_summed")
        s_dg, s_ts, s_x1, s_s2, s_ve2, s_rs2, s_rx2 = (sem(n) for n in (
            "degree_chain", "acc_read", "x1_made", "stats2_chain", "variance2", "rstd2", "scale2"))
        s_xh2, s_hi2, s_lo2, s_tp2, s_xT2, s_lgp = (sem(n) for n in (
            "normalised2", "hi2", "lo2", "transposed2", "transposed2_copied", "logits_product"))
        s_lg = sem("logits")
        s_rc, s_both, s_sl, s_rkp, s_slot = (sem(n) for n in ("route_chain", "one_hots", "slot_chain", "ranks", "slots"))
        s_id, s_sc = sem("pair_numbers"), [sem("first_dispatched"), sem("second_dispatched")]
        s_ew, s_emx, s_emr, s_ech, s_es, s_et, s_eh, s_el = (sem(n) for n in (
            "expert_weights_loaded", "expert_max", "expert_max_all", "expert_chain", "expert_scales", "expert_scaled",
            "expert_hi", "expert_lo"))
        s_tot, s_tch, s_tab, s_padw, s_dum = (sem(n) for n in (
            "totals", "table_chain", "tables", "pads_written", "dummies_written"))
        s_wd, s_wx, s_wc, s_wm = sem("logit_gap"), sem("gap_exp"), sem("mix_chain"), sem("mix_weights")
        s_er = [sem(f"expert_rows_loaded{i}") for i in range(R)]
        s_etp, s_idc, s_exT, s_ehp, s_eg, s_ehi, s_elo, s_eyp, s_ey = (sem(n) for n in (
            "e_transposed", "e_numbers_copied", "e_transposed_copied", "e_hidden_product", "e_hidden", "e_hidden_hi", "e_hidden_lo",
            "e_out_product", "e_out"))
        s_ysc = [sem(f"outputs_scattered{i}") for i in range(R)]
        s_yl, s_o1, s_o2, s_out = [sem("pairs_loaded0"), sem("pairs_loaded1")], sem("first_added"), sem("second_added"), sem("out_written")

        class Chain:

            def __init__(self, eng, s, base):
                self.eng, self.s, self.base, self.n = eng, s, base, 0

            def __call__(self, ins):
                self.n += 1
                ins.then_inc(self.s, 1)
                self.eng.wait_ge(self.s, self.base + self.n)

        def flat(a, t):
            return a[:, at(t), :].rearrange("p o n -> p (o n)")

        def spread(a, n=B):
            return a[:, :].rearrange("p (o e) -> p o e", o=1).to_broadcast((P, n, E))

        def at(t, n=1):
            return slice(t, t + n) if isinstance(t, int) else bass.ds(t, n)

        def div(t, u, known, lag, n):
            return (known - lag) // n if known is not None else (B // n) * kreg[0] + (u - lag) // n

        kreg = [None]

        X1, NORM, LOGIT, SCORE, HOT, SLOT = 3, 4, 6, 9, 12, 15
        EMAX, ESCALE, ESPLIT = 4, 5, 6
        GATE_STEPS = NT + SLOT - B + 1

        def steps(eng, step, peel, end, total=None, tail=0):
            total = NT if total is None else total
            for t in range(B * peel):
                step(t, t, t)
            with eng.Fori(peel, total // B - tail) as k:
                kreg[0] = k
                for e in range(B):
                    step(B * k + e, e, None)
            for t in range(total - B * tail, end):
                step(t, t, t)

        def live(known, lag, total=None):
            total = NT if total is None else total
            return known is None or 0 <= known - lag < total

        def write_pads(eng, to, n, s):
            to = to.rearrange("(p s) n -> p s n", s=2)
            eng.dma_start(to[:, :, 0:2 * D], pad[:, :, :]).then_inc(s, 16)
            eng.dma_start(to[:, :, 2 * D:RW].bitcast(I32).rearrange("p s o -> p (s o)"), padn[:, n, :],
                          allow_slow_non_contiguous=True).then_inc(s, 16)

        def load_experts(eng, held, lags, t, u, known):
            kept = {j: r for j, r in held.get("tiles", {}).items() if u > 0}
            held["tiles"] = {}
            for lag in lags:
                if live(known, lag, ET):
                    held[lag] = kept.get(u - lag)
                    if held[lag] is None:
                        held[lag] = eng.value_load(tab[0:1, 1, at(t - lag)], min_val=0, max_val=E - 1)
                    kept[u - lag] = held[lag]
            held["tiles"] = {j: r for j, r in kept.items() if j > u - max(lags)}

        def apart(eng):
            eng.nop(nofuse=True)

        block = ctx.enter_context(nc.Block())

        @block.sync
        def _(sp):
            def load_x(k, s):
                for g in range(G):
                    sp.dma_start(x_sb[Q * g:Q * g + Q, B * k:B * k + B, :].rearrange("p e d -> p (e d)"),
                                 x_v[g, k]).then_inc(s, 16)

            load_x(0, s_x[0])
            for w, m in enumerate((W_self, W_nb)):
                sp.dma_start(wraw[:, w], m.rearrange("(t p) n -> p t n", p=P)).then_inc(s_w, 16)
            sp.dma_start(wraw[:, 2:4].rearrange("p w t n -> p (w t) n"),
                         W_comb.rearrange("(t p) n -> p t n", p=P)).then_inc(s_w, 16)
            for k in range(1, NG):
                load_x(k, s_x[min(k, 3)])

            def load_adj(t, u, known):
                for h in range(2):
                    s = 2 * (u % 2) + h
                    if known is None or known >= 2:
                        sp.wait_ge((s_mD, s_mA)[h], t - 1)
                    for g in range(G):
                        if known is not None:
                            src = adj_v[t // B, t % B, g]
                        else:
                            src = adj_v[bass.ds(kreg[0], 1), u, g].rearrange("o r b j -> (o r) b j")
                        sp.dma_start(stage[Q * g:Q * g + Q, s], src[:, 2 * h:2 * h + 2, :]).then_inc(s_adj[s], 16)

            sp.wait_ge(s_cp, 1)
            sp.wait_ge(s_wf, 2)
            steps(sp, load_adj, 1, NT)

            sp.wait_ge(s_pad, 2)
            sp.wait_ge(s_tab, 2)
            for e in range(E):
                row = sp.value_load(padrow[0:1, e:e + 1], min_val=0, max_val=E * CAP - TT)
                write_pads(sp, xs_dram[bass.ds(row, TT), :], e, s_padw)
            sp.wait_ge(s_padw, 32 * E)
            sp.wait_ge(s_dum, 32 * DUM)
            for c in range(2):
                sp.wait_ge(s_sc[c], 16 * NT)

            def load_rows(t, u, known):
                a = u % R
                if known is None or known >= R:
                    sp.wait_ge(s_etp, t - R + 1)
                    sp.wait_ge(s_idc, t - R + 1)
                    apart(sp)
                row = sp.value_load(tab[0:1, 0, at(t)], min_val=0, max_val=E * CAP + (DUM - 1) * TT)
                sp.dma_start(erow[:, a], xs_dram[bass.ds(row, TT), :].rearrange("(p s) n -> p s n", s=2)).then_inc(s_er[a], 16)

            steps(sp, load_rows, 1, ET, ET)

            for a in range(R):
                sp.wait_ge(s_ysc[a], 32 * (ET // R))
            def load_pairs(k, par, first):
                if not first:
                    sp.wait_ge(s_o2, B * (k - 1))
                    apart(sp)
                for g in range(G):
                    src = yp_v[g, k] if first else yp_v[g, at(k)].rearrange("o c n -> (o c) n")
                    sp.dma_start(yin[Q * g:Q * g + Q, par].rearrange("p e k n -> p (e k n)"), src).then_inc(s_yl[par], 16)

            for k in range(2):
                load_pairs(k, k, True)
            with sp.Fori(1, NG // 2) as kk:
                for par in range(2):
                    load_pairs(2 * kk + par, par, False)
            sp.wait_ge(s_out, 16 * G * NG)

        @block.gpsimd
        def _(pool):
            gp = nc.gpsimd
            pool.dma_start(bcol[:, 0, :], b_self.rearrange("(t p) -> p t", p=P), allow_slow_non_contiguous=True).then_inc(s_small, 16)
            pool.dma_start(bcol[:, 1, :], b_nb.rearrange("(t p) -> p t", p=P), allow_slow_non_contiguous=True).then_inc(s_small, 16)
            pool.dma_start(bc_bc[:, :], b_comb.rearrange("(o n) -> o n", o=1).to_broadcast((P, D))).then_inc(s_small, 16)
            pool.dma_start(bg_bc[:, :], bg.rearrange("(o n) -> o n", o=1).to_broadcast((P, E))).then_inc(s_small, 16)
            pool.dma_start(wg_f[:, :, :], Wg.rearrange("(t p) n -> p t n", p=P)).then_inc(s_small, 16)
            gp.iota(diff[:, :], [[1, P]], base=0, channel_multiplier=-1).then_inc(s_io, 1)
            gp.memset(mhalf[:, :], -0.5).then_inc(s_io, 1)
            small = dict(channel_multiplier=0, allow_small_or_imprecise_dtypes=True)
            gp.iota(iota8[:, :], [[1, E]], base=0, **small).then_inc(s_io, 1)
            gp.iota(region[:, :], [[CAP, E]], base=0, **small).then_inc(s_io, 1)
            for g in range(G):
                pool.wait_ge(s_io, 4 + g)
                gp.iota(pid[Q * g:Q * g + Q, :, :], [[2 * P, NG], [2, B], [1, 2]], base=2 * NQ * g,
                        channel_multiplier=2 * B).then_inc(s_io, 1)
            pool.wait_ge(s_io, 8)
            gp.memset(pad[:, :, :], 0.0).then_inc(s_pad, 1)
            gp.iota(padn[:, :, :], [[TT, E + DUM], [1, 2]], base=2 * N, channel_multiplier=2).then_inc(s_pad, 1)
            def rstd(k):
                pool.wait_ge(s_ve, k + 1)
                gp.tensor_tensor(rs[:, 0, B * k:B * k + B], ve[:, 0, B * k:B * k + B], mhalf[:, :], ALU.pow).then_inc(s_rs, 1)

            rstd(0)
            pool.wait_ge(s_fmx, 2)
            gp.partition_all_reduce(fmr[:, :], fmx[:, :], P, RED.absmax).then_inc(s_fmr, 1)
            for k in range(1, NG):
                rstd(k)
            for e in range(E):
                pool.dma_start(b1c[:, e, :], b1[e].rearrange("(t p) -> p t", p=P), allow_slow_non_contiguous=True).then_inc(s_b12, 16)
            pool.wait_ge(s_pad, 2)
            for q in range(DUM):
                write_pads(pool, xs_dram[E * CAP + q * TT:E * CAP + (q + 1) * TT, :], E + q, s_dum)

            def expert_load(k):
                if k:
                    pool.wait_ge(s_el, 2 * k)
                for w, m in enumerate((W1, W2)):
                    pool.dma_start(wst[:, w], m[k].rearrange("(t p) n -> p t n", p=P)).then_inc(s_ew, 16)

            def expert_max(k):
                pool.wait_ge(s_emx, k + 1)
                gp.partition_all_reduce(emr[:, :], emx[:, :], P, RED.absmax).then_inc(s_emr, 1)

            def expert_scale(k):
                pool.wait_ge(s_es, k + 1)
                for w in range(2):
                    gp.tensor_scalar(wst[:, w], wst[:, w], s12[:, w:w + 1], None, ALU.mult).then_inc(s_et, 1)

            def expert_split(k):
                pool.wait_ge(s_et, 2 * k + 2)
                for w in range(2):
                    gp.tensor_copy(w12[:, k, w, 0], wst[:, w]).then_inc(s_eh, 1)
                pool.wait_ge(s_eh, 2 * k + 2)
                for w in range(2):
                    gp.tensor_tensor(w12[:, k, w, 1], wst[:, w], w12[:, k, w, 0], ALU.subtract).then_inc(s_el, 1)

            def numbers(k, c):
                gp.tensor_copy(self_sb[:, B * k:B * k + B, D:D + 1].bitcast(I32), pid[:, B * k:B * k + B, c:c + 1]).then_inc(s_id, 1)

            def dispatch(k, c):
                if c == 0:
                    pool.wait_ge(s_lo2, B * k + B)
                    pool.wait_ge(s_hi2, B * k + B)
                    pool.wait_ge(s_slot, k + 1)
                else:
                    pool.wait_ge(s_sc[0], 16 * B * (k + 1))
                numbers(k, c)
                pool.wait_ge(s_id, 2 * k + c + 1)
                for t in range(B * k, B * k + B):
                    gp.indirect_dma_start(
                        out=xs_dram[:, :], out_offset=bass.IndirectOffsetOnAxis(ap=slot[:, t, c:c + 1], axis=0),
                        in_=self_sb[:, t, :].bitcast(F16), in_offset=None).then_inc(s_sc[c], 16)

            expert_load(0)
            for s in range(GATE_STEPS + 1):
                if 0 <= s - X1 < NT:
                    t = s - X1
                    pool.wait_ge(s_ve2, t + 1)
                    gp.tensor_tensor(rs[:, 1, t:t + 1], ve[:, 1, t:t + 1], mhalf[:, 0:1], ALU.pow).then_inc(s_rs2, 1)
                for lag, part in ((EMAX, expert_max), (ESCALE, expert_scale), (ESPLIT, expert_split)):
                    if 0 <= s - lag < NT and (s - lag) % B == 0:
                        part((s - lag) // B)
                        if part is expert_split and s - lag + B < NT:
                            expert_load((s - lag) // B + 1)
                if s == NT + X1:
                    pool.wait_ge(s_mm, NT)
                    gp.iota(q256[:, :, :], [[0, E], [TT, N // TT]], base=0, **small).then_inc(s_iot, 1)
                    gp.iota(tio[:, :, :], [[1, ET], [0, E]], base=0, **small).then_inc(s_iot, 1)
                    pool.dma_start(b2_bc[:, :, :].rearrange("p e n -> p (e n)"),
                                   b2.rearrange("(o e) n -> o (e n)", o=1).to_broadcast((P, E * H))).then_inc(s_b2, 16)
                if s >= SLOT and s % B == SLOT % B:
                    dispatch((s - SLOT) // B, 0)
                if s > SLOT and s % B == (SLOT + 1) % B:
                    dispatch((s - SLOT) // B, 1)

            def scatter(t, u, known):
                if live(known, 3, ET):
                    a = (u - 3) % R
                    pool.wait_ge(s_idc, t - 2)
                    pool.wait_ge(s_ey, t - 2)
                    apart(pool)
                    for s in range(2):
                        gp.indirect_dma_start(
                            out=yp_dram[:, :], out_offset=bass.IndirectOffsetOnAxis(ap=enum[:, a, s:s + 1], axis=0),
                            in_=ysb[:, a, s, :], in_offset=None).then_inc(s_ysc[a], 16)
                if live(known, 0, ET):
                    a = u % R
                    if known is None or known >= R:
                        pool.wait_ge(s_ysc[a], 32 * div(t, u, known, 0, R))
                    pool.wait_ge(s_er[a], 16 * (div(t, u, known, 0, R) + 1))
                    apart(pool)
                    gp.tensor_copy(enum[:, a, :], erow[:, a, :, 2 * D:RW].bitcast(I32).rearrange("p s o -> p (s o)")).then_inc(s_idc, 1)

            steps(pool, scatter, 1, ET + 3, ET)

        @block.scalar
        def _(act):
            sc = nc.scalar

            def setup_step(t, u, known):
                if live(known, 0):
                    if known is None or known >= 2:
                        act.wait_ge(s_lo, t - 1)
                    act.wait_ge(s_nb, div(t, u, known, 0, B) + 1)
                    sc.activation(xh[:, u % 2, :], flat(x_sb, t), ACT.Identity, bias=nbx[:, at(t)],
                                  scale=rs[:, 0, at(t)]).then_inc(s_xh, 1)
                    if known is None or known >= 4:
                        act.wait_ge(s_tp, t - 3)
                    act.wait_ge(s_xh, t + 1)
                    sc.copy(hl[:, u % 4, 0:D], xh[:, u % 2, :]).then_inc(s_hi, 1)
                if live(known, 2):
                    act.wait_ge(s_tp, t - 1)
                    if known is None or known >= 6:
                        act.wait_ge(s_zp, t - 5)
                    sc.copy(xT[:, (u - 2) % 4, :], tp16[(u - 2) % 2]).then_inc(s_xT, 1)
                if live(known, 4):
                    act.wait_ge(s_zp, t - 3)
                    sc.mul(z_hi[:, at(t - 4), 0:D].rearrange("p o d -> p (o d)"), zbank[(u - 4) % 4][:, D:2 * D],
                           2.0 ** -19).then_inc(s_zhi, 1)

            steps(act, setup_step, 2, NT + 4)

            def main_step(t, u, known):
                if live(known, 0):
                    s = 2 * (u % 2) + 1
                    act.wait_ge(s_adj[s], 64 * (div(t, u, known, 0, 2) + 1))
                    if known is None or known >= 2:
                        act.wait_ge(s_T, t - 1)
                    apart(act)
                    sc.activation(mask[:, u % 2, 2:4, :], stage[:, s], ACT.Sigmoid, bias=m100[:, 0:1], scale=200.0,
                                  saturate=False).then_inc(s_mA, 1)
                if live(known, NORM):
                    act.wait_ge(s_xh2, t - NORM + 1)
                    sc.copy(row16[:, at(t - NORM), 0:D].rearrange("p o d -> p (o d)"), xh[:, (u - NORM) % 2, :]).then_inc(s_hi2, 1)
                if live(known, LOGIT):
                    act.wait_ge(s_tp2, t - LOGIT + 1)
                    if known is None or known - LOGIT >= 4:
                        act.wait_ge(s_lgp, t - LOGIT - 3)
                    sc.copy(xT[:, (u - LOGIT) % 4, :], tps[(u - LOGIT) % 2][:, :]).then_inc(s_xT2, 1)

            act.wait_ge(s_cst, 1)
            act.wait_ge(s_zp, NT)
            steps(act, main_step, 3, NT + LOGIT)

            act.wait_ge(s_wd, 1)
            sc.activation(wexp[:, :], wdif[:, :], ACT.Exp).then_inc(s_wx, 1)

            def expert_step(t, u, known):
                ex = act.value_load(tab[0:1, 1, at(t)], min_val=0, max_val=E - 1)
                if known is None or known >= 2:
                    act.wait_ge(s_elo, t - 1)
                for h in range(KT):
                    act.wait_ge(s_ehp, 2 * t + h + 1)
                    sc.activation(ehid[:, u % 2, h, :], hps[2 * (u % 2) + h][:, 0:TT], ACT.Gelu,
                                  bias=b1c[:, bass.ds(ex, 1), h], scale=sc1[:, bass.ds(ex, 1)]).then_inc(s_eg, 1)
                act.wait_ge(s_eg, 2 * t + 2)
                if known is None or known >= 2:
                    act.wait_ge(s_eyp, t - 1)
                sc.activation(ehl[:, u % 2, 0].rearrange("p t n -> p (t n)"), ehid[:, u % 2].rearrange("p t n -> p (t n)"),
                              ACT.Copy, scale=shs[:, bass.ds(ex, 1)]).then_inc(s_ehi, 1)

            act.wait_ge(s_tab, 2)
            act.wait_ge(s_b12, 16 * E)
            steps(act, expert_step, 1, ET, ET)

            with act.Fori(0, NG) as k:
                act.wait_ge(s_o2, B * k + B)
                for g in range(G):
                    act.dma_start(out_v[g, bass.ds(k, 1)].rearrange("o c n -> (o c) n"),
                                  x_sb[Q * g:Q * g + Q, bass.ds(B * k, B), :].rearrange("p e d -> p (e d)")).then_inc(s_out, 16)

        @block.vector
        def _(dve):
            v = nc.vector

            def stats_a(k):
                for e in range(B):
                    v.bn_stats(st6[:, 0, e, :], flat(x_sb, B * k + e)).then_inc(s_st, 1)
                dve.wait_ge(s_st, 2 * B * k + B)
                for e in range(B):
                    if e == 0:
                        apart(dve)
                    v.bn_aggr(mv[:, e, :], st6[:, 0, e, :]).then_inc(s_st, 1)
                dve.wait_ge(s_st, 2 * B * (k + 1))
                v.tensor_scalar(ve[:, 0, at(B * k, B)], mv[:, :, 1],
                                EPS, XS ** -2, ALU.add, ALU.mult).then_inc(s_ve, 1)

            def stats_b(k):
                dve.wait_ge(s_rs, k + 1)
                v.scalar_tensor_tensor(nbx[:, at(B * k, B)], mv[:, :, 0],
                                       -1.0, rs[:, 0, at(B * k, B)], ALU.mult, ALU.mult).then_inc(s_nb, 1)

            def powers(ch, out_, inv, mx):
                ch(v.tensor_scalar(mx, mx, 1e-30, None, ALU.max))
                ch(v.tensor_scalar(out_.bitcast(U32), mx.bitcast(U32), 0x7F800000, None, ALU.bitwise_and))
                ch(v.reciprocal(inv, out_))

            dve.wait_ge(s_io, 8)
            v.tensor_scalar(identf[:, :], diff[:, :], 0.0, None, ALU.is_equal).then_inc(s_idt, 1)
            v.tensor_scalar(ident[:, :], diff[:, :], 0.0, None, ALU.is_equal).then_inc(s_idt, 1)
            v.tensor_scalar(upper[:, :], diff[:, :], 0.0, None, ALU.is_gt).then_inc(s_idt, 1)
            v.memset(ones[:, :], 1.0).then_inc(s_idt, 1)
            v.memset(m100[:, :], -100.0).then_inc(s_cst, 1)
            v.memset(onesE[:, :], 1.0).then_inc(s_cst, 1)
            v.memset(z_hi[:, :, D:D + 1], 1.0).then_inc(s_cst, 1)
            v.memset(base[:, :, :], 0.0).then_inc(s_cst, 1)
            dve.wait_ge(s_x[0], 16 * G)
            stats_a(0)

            for w in range(2):
                dve.wait_ge(s_wtp, w + 1)
                v.tensor_copy(wT[:, w].rearrange("p t n -> p (t n)"), wps[w][:, :]).then_inc(s_wtc, 1)
            dve.wait_ge(s_small, 16 * 5)
            dve.wait_ge(s_idt, 4)
            for w in range(2):
                for t in range(KT):
                    v.tensor_scalar(bbig[:, w, t, :], ones[:, :], bcol[:, w, t:t + 1], None, ALU.mult).then_inc(s_bb, 1)
            stats_b(0)
            dve.wait_ge(s_fold, 1)
            for t in range(KT):
                v.tensor_copy(wsum[:, t, :], fold[t][:, :]).then_inc(s_wsum, 1)
            dve.wait_ge(s_wsum, KT)
            v.tensor_reduce(fmx[:, 0:1], wsum[:, :, :].rearrange("p t n -> p (t n)"), AX.X, ALU.max, apply_absolute_value=True).then_inc(s_fmx, 1)
            v.tensor_reduce(fmx[:, 1:2], wg_f[:, :, :].rearrange("p t n -> p (t n)"), AX.X, ALU.max, apply_absolute_value=True).then_inc(s_fmx, 1)
            dve.wait_ge(s_cp, 1)
            v.tensor_tensor(const_bc[:, :], cbank[:, 0:D], bc_bc[:, :], ALU.add).then_inc(s_cb, 1)
            dve.wait_ge(s_fmr, 1)
            ch = Chain(dve, s_fch, 0)
            powers(ch, fp2[:, :], fin[:, :], fmr[:, :])
            ch(v.tensor_scalar(scw[:, 0:2], fin[:, :], 2.0 ** 14, None, ALU.mult))
            ch(v.tensor_scalar(scw[:, 2:4], fp2[:, :], 2.0 ** -14 / XS, None, ALU.mult))
            ch(v.tensor_scalar(scw[:, 4:5], fin[:, 0:1], 2.0 ** 6, None, ALU.mult))
            for out_, in_, c in ((wf, wsum, 0), (wg_s, wg_f, 1)):
                v.tensor_scalar(out_[:, 0], in_[:, :, :], scw[:, c:c + 1], None, ALU.mult).then_inc(s_wf, 1)
                dve.wait_ge(s_wf, 2 * c + 1)
                v.scalar_tensor_tensor(out_[:, 1], in_[:, :, :], scw[:, c:c + 1], out_[:, 0], ALU.mult, ALU.subtract).then_inc(s_wf, 1)

            def setup_step(t, u, known):
                nxt = div(t, u, known, 0, B) + 1
                if u % B == 0 and (known is None or known + B < NT):
                    if known is not None and nxt < 3:
                        dve.wait_ge(s_x[nxt], 16 * G)
                    else:
                        dve.wait_ge(s_x[3], 16 * G * (NG - 3))
                    stats_a(nxt)
                if live(known, 5):
                    b_ = zbank[(u - 5) % 4]
                    dve.wait_ge(s_zhi, t - 4)
                    v.scalar_tensor_tensor(flat(z_lo, t - 5), b_[:, D:2 * D], 2.0 ** -19,
                                           z_hi[:, at(t - 5), 0:D].rearrange("p o d -> p (o d)"),
                                           ALU.mult, ALU.subtract).then_inc(s_zlo, 1)
                    v.scalar_tensor_tensor(self_sb[:, at(t - 5), 0:D].rearrange("p o d -> p (o d)"), b_[:, 0:D],
                                           scw[:, 2:3], const_bc[:, :], ALU.mult, ALU.add).then_inc(s_self, 1)
                if u % B == 2 and (known is None or known + B - 2 < NT):
                    stats_b(nxt)
                if live(known, 0):
                    dve.wait_ge(s_hi, t + 1)
                    v.tensor_tensor(hl[:, u % 4, D:2 * D], xh[:, u % 2, :], hl[:, u % 4, 0:D], ALU.subtract).then_inc(s_lo, 1)

            dve.wait_ge(s_cb, 1)
            steps(dve, setup_step, 2, NT + 5, tail=1)

            def main_step(t, u, known):
                if live(known, NORM):
                    j = t - NORM
                    dve.wait_ge(s_rs2, j + 1)
                    if known is None or known - NORM >= 2:
                        dve.wait_ge(s_hi2, j - 1)
                    v.tensor_scalar(xh[:, (u - NORM) % 2, :], flat(x_sb, j), mv2[:, (u - NORM) % 4, 0:1], rs[:, 1, at(j)],
                                    ALU.subtract, ALU.mult).then_inc(s_xh2, 1)
                if live(known, X1):
                    j, p, r = t - X1, acc[(u - X1) % 2], (u - X1) % 4
                    dve.wait_ge(s_mm, j + 1)
                    v.tensor_scalar(sdeg[:, r:r + 1], p[:, D:D + 1], 1.0, scw[:, 4:5], ALU.max, ALU.mult).then_inc(s_dg, 1)
                if live(known, 0):
                    s = 2 * (u % 2)
                    dve.wait_ge(s_adj[s], 64 * (div(t, u, known, 0, 2) + 1))
                    apart(dve)
                    v.tensor_scalar(mask[:, u % 2, 0:2, :], stage[:, s], 0.0, None, ALU.is_gt, saturate=False).then_inc(s_mD, 1)
                if live(known, X1):
                    dve.wait_ge(s_dg, 2 * j + 1)
                    v.reciprocal(rdeg[:, r:r + 1], sdeg[:, r:r + 1]).then_inc(s_dg, 1)
                    dve.wait_ge(s_dg, 2 * j + 2)
                    v.scalar_tensor_tensor(tsum[:, r % 2, :], p[:, 0:D], rdeg[:, r:r + 1],
                                           self_sb[:, at(j), 0:D].rearrange("p o d -> p (o d)"), ALU.mult, ALU.add).then_inc(s_ts, 1)
                if live(known, NORM):
                    i = t - NORM
                    dve.wait_ge(s_hi2, i + 1)
                    v.tensor_tensor(row16[:, at(i), D:2 * D].rearrange("p o d -> p (o d)"), xh[:, (u - NORM) % 2, :],
                                    row16[:, at(i), 0:D].rearrange("p o d -> p (o d)"), ALU.subtract).then_inc(s_lo2, 1)
                if live(known, X1):
                    dve.wait_ge(s_ts, j + 1)
                    v.scalar_tensor_tensor(flat(x_sb, j), tsum[:, r % 2, :], 0.0, flat(x_sb, j), ALU.max, ALU.add).then_inc(s_x1, 1)
                if live(known, 0):
                    dve.wait_ge(s_mD, t + 1)
                    dve.wait_ge(s_mA, t + 1)
                    if known is None or known >= 4:
                        dve.wait_ge(s_mm, t - 3)
                    v.transpose(maskT32[u % 4], mask32[u % 2]).then_inc(s_T, 1)
                if live(known, X1):
                    dve.wait_ge(s_x1, j + 1)
                    apart(dve)
                    v.bn_stats(st6[:, 1, r, :], flat(x_sb, j)).then_inc(s_s2, 1)
                    dve.wait_ge(s_s2, 2 * j + 1)
                    apart(dve)
                    v.bn_aggr(mv2[:, r, :], st6[:, 1, r, :]).then_inc(s_s2, 1)
                    dve.wait_ge(s_s2, 2 * j + 2)
                    v.tensor_scalar(ve[:, 1, at(j)], mv2[:, r, 1:2], EPS, XS ** -2, ALU.add, ALU.mult).then_inc(s_ve2, 1)
                if u % B == EMAX % B and live(known, EMAX):
                    expert_max(div(t, u, known, EMAX, B))
                if u % B == ESCALE % B and live(known, ESCALE):
                    expert_scales(div(t, u, known, ESCALE, B))
                if live(known, SCORE):
                    i = t - SCORE
                    dve.wait_ge(s_lgp, i + 1)
                    v.scalar_tensor_tensor(lg[:, (u - SCORE) % B, :], lbank[(u - SCORE) % 2][:, 0:E], scw[:, 3:4], bg_bc[:, :],
                                           ALU.mult, ALU.add).then_inc(s_lg, 1)
                if u % B == HOT % B and live(known, HOT):
                    choose(div(t, u, known, HOT, B))
                if u % B == SLOT % B and live(known, SLOT):
                    slots(div(t, u, known, SLOT, B))

            def expert_max(k):
                dve.wait_ge(s_ew, 32 * (k + 1))
                dve.wait_ge(s_b12, 16 * E)
                for w in range(2):
                    v.tensor_reduce(emx[:, w:w + 1], wst[:, w].rearrange("p t n -> p (t n)"), AX.X, ALU.max, apply_absolute_value=True)
                v.tensor_reduce(emx[:, 2:3], flat(b1c, k), AX.X, ALU.max, apply_absolute_value=True).then_inc(s_emx, 1)

            def expert_scales(k):
                dve.wait_ge(s_emr, k + 1)
                ch = Chain(dve, s_ech, 4 * k)
                v.tensor_copy(ecl[:, 0:2], emr[:, 0:2])
                ch(v.scalar_tensor_tensor(ecl[:, 2:3], emr[:, 0:1], float(D), emr[:, 2:3], ALU.mult, ALU.add))
                powers(ch, ep2[:, :], ein[:, :], ecl[:, :])
                v.tensor_scalar(sc1[:, at(k)], ep2[:, 0:1], 2.0 ** -14 / XS, None, ALU.mult)
                v.tensor_scalar(shs[:, at(k)], ein[:, 2:3], 2.0 ** 14, None, ALU.mult)
                v.scalar_tensor_tensor(sc2[:, at(k)], ep2[:, 2:3], 2.0 ** -28, ep2[:, 1:2], ALU.mult, ALU.mult)
                v.tensor_scalar(s12[:, :], ein[:, 0:2], 2.0 ** 14, None, ALU.mult).then_inc(s_es, 1)

            def choose(k):
                dve.wait_ge(s_lg, B * (k + 1))
                if not isinstance(k, int) or k:
                    dve.wait_ge(s_both, k)
                ch = Chain(dve, s_rc, HN * k)
                apart(dve)
                for b_ in range(B):
                    last = v.max(top[:, b_, :], lg[:, b_, :])
                ch(last)
                v.tensor_copy(m12[:, at(B * k, B), :], top[:, :, 0:2])
                for b_ in range(B):
                    last = v.max_index(tidx[:, b_, :], top[:, b_, :], lg[:, b_, :])
                ch(last)
                ch(v.tensor_copy(tidf[:, :, :], tidx[:, :, 0:2]))
                for c in range(2):
                    last = v.tensor_tensor(hot[:, c], spread(iota8), tidf[:, :, c:c + 1].to_broadcast((P, B, E)), ALU.is_equal)
                ch(last)
                ch(v.tensor_tensor(both[:, :, :], hot[:, 0], hot[:, 1], ALU.add))
                ch(v.tensor_copy(base[:, 0, :], base[:, B, :]))
                for b_ in range(B - 1):
                    ch(v.tensor_tensor(base[:, b_ + 1, :], base[:, b_, :], both[:, b_, :], ALU.add))
                v.tensor_tensor(base[:, B, :], base[:, B - 1, :], both[:, B - 1, :], ALU.add).then_inc(s_both, 1)
                assert ch.n == HN

            HN = 6 + B - 1

            def slots(k):
                dve.wait_ge(s_rkp, k + 1)
                ch = Chain(dve, s_sl, 3 * k)
                ch(v.tensor_tensor(rk[:, :, :], rbank[:, 0:B * E].rearrange("p (b e) -> p b e", b=B), spread(region), ALU.add))
                for c in range(2):
                    last = v.tensor_tensor(pick[:, c], hot[:, c], rk[:, :, :], ALU.mult)
                ch(last)
                ch(v.tensor_reduce(slotf[:, :, :], pick[:, :, :, :], AX.X, ALU.add))
                v.tensor_copy(slot[:, at(B * k, B), :].rearrange("p t c -> p c t"), slotf[:, :, :]).then_inc(s_slot, 1)

            steps(dve, main_step, 4, GATE_STEPS + 1)

            dve.wait_ge(s_tot, 1)
            dve.wait_ge(s_iot, 2)
            ch = Chain(dve, s_tch, 0)
            ch(v.tensor_copy(cntt[:, :], tbank[:, 0:E]))
            ch(v.tensor_tensor(cmpq[:, :, :], cntt[:, :].rearrange("p (e o) -> p e o", o=1).to_broadcast((P, E, N // TT)), q256[:, :, :], ALU.is_gt))
            ch(v.tensor_reduce(nti[:, :], cmpq[:, :, :], AX.X, ALU.add))
            ch(v.tensor_tensor_scan(cinc[:, :], onesE[:, :], nti[:, :], 0.0, ALU.mult, ALU.add))
            ch(v.tensor_scalar(coef[:, :], nti[:, :], -float(TT), float(CAP), ALU.mult, ALU.add))
            ch(v.tensor_tensor(tge[:, :, :], tio[:, :, :], spread(cinc, ET), ALU.is_ge))
            ch(v.tensor_tensor(tgc[:, :, :], tge[:, :, :], spread(coef, ET), ALU.mult))
            ch(v.tensor_reduce(tjmp[:, :], tgc[:, :, :], AX.X, ALU.add))
            ch(v.tensor_reduce(texp[:, :], tge[:, :, :], AX.X, ALU.add))
            v.scalar_tensor_tensor(tab[:, 0, :], tio[:, :, 0], float(TT), tjmp[:, :], ALU.mult, ALU.add)
            v.tensor_scalar(tab[:, 1, :], texp[:, :], float(E - 1), None, ALU.min).then_inc(s_tab, 1)
            v.tensor_tensor(padrow[:, :], cntt[:, :], region[:, :], ALU.add).then_inc(s_tab, 1)
            v.tensor_tensor(wdif[:, :], m12[:, :, 1], m12[:, :, 0], ALU.subtract).then_inc(s_wd, 1)
            dve.wait_ge(s_wx, 1)
            ch(v.tensor_scalar(wden[:, :], wexp[:, :], 1.0, None, ALU.add))
            ch(v.reciprocal(wts[:, 0, :], wden[:, :]))
            v.tensor_tensor(wts[:, 1, :], wexp[:, :], wts[:, 0, :], ALU.mult).then_inc(s_wm, 1)

            expert_of = {}

            def expert_step(t, u, known):
                load_experts(dve, expert_of, (1, 3), t, u, known)
                if live(known, 0, ET):
                    dve.wait_ge(s_etp, t + 1)
                    if known is None or known >= 2:
                        dve.wait_ge(s_ehp, 2 * t - 2)
                    v.tensor_copy(exT[:, u % 2, :], etp16[u % 2]).then_inc(s_exT, 1)
                if live(known, 3, ET):
                    j, a, ex = t - 3, (u - 3) % R, expert_of[3]
                    dve.wait_ge(s_eyp, j + 1)
                    if known is None or known - 3 >= R:
                        dve.wait_ge(s_ysc[a], 32 * div(t, u, known, 3, R))
                    v.scalar_tensor_tensor(ysb[:, a, :, :], fold[(u - 3) % 2][:, :].rearrange("p (s n) -> p s n", s=2),
                                           sc2[:, bass.ds(ex, 1)], b2_bc[:, bass.ds(ex, 1), :].to_broadcast((P, 2, H)),
                                           ALU.mult, ALU.add).then_inc(s_ey, 1)
                if live(known, 1, ET):
                    j, r, ex = t - 1, (u - 1) % 2, expert_of[1]
                    dve.wait_ge(s_ehi, j + 1)
                    v.scalar_tensor_tensor(ehl[:, r, 1].rearrange("p t n -> p (t n)"), ehid[:, r].rearrange("p t n -> p (t n)"),
                                           shs[:, bass.ds(ex, 1)], ehl[:, r, 0].rearrange("p t n -> p (t n)"),
                                           ALU.mult, ALU.subtract).then_inc(s_elo, 1)

            dve.wait_ge(s_b2, 16)
            steps(dve, expert_step, 2, ET + 3, ET)

            def combine(k, kk, par):
                dve.wait_ge(s_yl[par], 16 * G * (kk + 1))
                for e in range(B):
                    t = B * k + e
                    v.scalar_tensor_tensor(flat(x_sb, t), yin[:, par, e, 0, :], wts[:, 0, at(t)], flat(x_sb, t), ALU.mult, ALU.add).then_inc(s_o1, 1)
                for e in range(B):
                    t = B * k + e
                    dve.wait_ge(s_o1, B * (k + 1))
                    v.scalar_tensor_tensor(flat(x_sb, t), yin[:, par, e, 1, :], wts[:, 1, at(t)], flat(x_sb, t), ALU.mult, ALU.add).then_inc(s_o2, 1)

            dve.wait_ge(s_wm, 1)
            with dve.Fori(0, NG // 2) as kk:
                for par in range(2):
                    combine(2 * kk + par, kk, par)

        @block.tensor
        def _(pe):
            mm = nc.tensor.matmul
            PARTS = ((0, 0), (1, 0), (0, 1))

            pe.wait_ge(s_idt, 1)
            pe.wait_ge(s_w, 48)
            for w in range(2):
                for kt in range(KT):
                    for dt in range(KT):
                        last = nc.tensor.transpose(wps[w][:, kt * D + dt * P:kt * D + dt * P + P],
                                                   wraw[:, w, dt, kt * P:kt * P + P], identf[:, :])
                last.then_inc(s_wtp, 1)
            pe.wait_ge(s_wtc, 2)
            for dt in range(KT):
                for w in range(2):
                    for kt in range(KT):
                        last = mm(fold[dt][:, w * D:w * D + D], wT[:, w, kt, dt * P:dt * P + P], wraw[:, 2 + w, kt, :],
                                  start=(kt == 0), stop=(kt == KT - 1))
            last.then_inc(s_fold, 1)
            pe.wait_ge(s_bb, 2 * KT)
            for w in range(2):
                for kt in range(KT):
                    last = mm(cbank[:, 0:D], bbig[:, w, kt, :], wraw[:, 2 + w, kt, :],
                              start=(w + kt == 0), stop=(w + kt == KT))
            last.then_inc(s_cp, 1)

            def setup_step(t, u, known):
                if live(known, 1):
                    j, b_ = t - 1, tp16[(u - 1) % 2]
                    pe.wait_ge(s_lo, t)
                    if known is None or known >= 3:
                        pe.wait_ge(s_xT, t - 2)
                    for q in range(2 * KT):
                        last = nc.tensor.transpose(b_[:, q * P:q * P + P], hl[:, (u - 1) % 4, q * P:q * P + P], ident[:, :])
                    last.then_inc(s_tp, 1)
                if live(known, 3):
                    pe.wait_ge(s_xT, t - 2)
                    if known is None or known >= 7:
                        pe.wait_ge(s_self, t - 6)
                    n = 0
                    for xp, wp in PARTS:
                        for kt in range(KT):
                            last = mm(zbank[(u - 3) % 4][:, :], xT[:, (u - 3) % 4, (xp * KT + kt) * P:(xp * KT + kt + 1) * P],
                                      wf[:, wp, kt, :], start=(n == 0), stop=(n == 3 * KT - 1))
                            n += 1
                    last.then_inc(s_zp, 1)

            pe.wait_ge(s_idt, 2)
            pe.wait_ge(s_wf, 2)
            pe.wait_ge(s_wsum, KT)
            steps(pe, setup_step, 2, NT + 3)

            def neighbours(u, half):
                n = NT // 2
                for i in range(n * half, n * half + n):
                    a = maskT8[u % 4][:, i // B, :, i % B]
                    mm(acc[u % 2][:, 0:D + 1], a, z_hi[:, i, :], start=(i == 0), stop=False)
                    last = mm(acc[u % 2][:, 0:D], a, z_lo[:, i, :], start=False, stop=(i == NT - 1))
                return last

            def main_step(t, u, known):
                if live(known, 0):
                    pe.wait_ge(s_T, t + 1)
                    if known is None or known >= 2:
                        pe.wait_ge(s_ts, t - 1)
                    apart(pe)
                    neighbours(u, 0)
                if live(known, NORM):
                    j = t - NORM
                    pe.wait_ge(s_lo2, j + 1)
                    if known is None or known - NORM >= 2:
                        pe.wait_ge(s_xT2, j - 1)
                    for q in range(2 * KT):
                        last = mm(tps[(u - NORM) % 2][:, q * P:q * P + P],
                                  row16[:, at(j), q * P:q * P + P].rearrange("p o d -> p (o d)"), ident[:, :],
                                  start=True, stop=True)
                    last.then_inc(s_tp2, 1)
                if live(known, 0):
                    neighbours(u, 1).then_inc(s_mm, 1)
                if live(known, LOGIT):
                    j = t - LOGIT
                    pe.wait_ge(s_xT2, j + 1)
                    if known is None or known - LOGIT >= 2:
                        pe.wait_ge(s_lg, j - 1)
                    n = 0
                    for xp, wp in PARTS:
                        for kt in range(KT):
                            last = mm(lbank[(u - LOGIT) % 2][:, 0:E], xT[:, (u - LOGIT) % 4, (xp * KT + kt) * P:(xp * KT + kt + 1) * P],
                                      wg_s[:, wp, kt, :], start=(n == 0), stop=(n == 3 * KT - 1))
                            n += 1
                    last.then_inc(s_lgp, 1)
                if u % B == HOT % B and live(known, HOT):
                    k = div(t, u, known, HOT, B)
                    pe.wait_ge(s_both, k + 1)
                    mm(rbank[:, 0:B * E], upper[:, :], both[:, :, :].rearrange("p b e -> p (b e)"), start=True, stop=False)
                    mm(rbank[:, 0:B * E], ones[:, :], base[:, 0:B, :].rearrange("p b e -> p (b e)"), start=False, stop=True).then_inc(s_rkp, 1)

            pe.wait_ge(s_self, NT)
            pe.wait_ge(s_zlo, NT)
            pe.wait_ge(s_xT, NT)
            pe.wait_ge(s_cst, 4)
            pe.wait_ge(s_wf, 4)
            pe.wait_ge(s_cb, 1)
            steps(pe, main_step, 3, NT + HOT - B + 1)
            mm(tbank[:, 0:E], ones[:, :], base[:, B, :], start=True, stop=True).then_inc(s_tot, 1)

            expert_of = {}

            def expert_step(t, u, known):
                load_experts(pe, expert_of, (1, 2), t, u, known)
                if live(known, 0, ET):
                    a = u % R
                    pe.wait_ge(s_er[a], 16 * (div(t, u, known, 0, R) + 1))
                    if known is None or known >= 2:
                        pe.wait_ge(s_exT, t - 1)
                    for q in range(2 * KT):
                        for s in range(2):
                            last = nc.tensor.transpose(etp16[u % 2][:, q * TT + s * P:q * TT + s * P + P],
                                                       erow[:, a, s, q * P:q * P + P], ident[:, :])
                    last.then_inc(s_etp, 1)
                if live(known, 1, ET):
                    j, r = t - 1, (u - 1) % 2
                    pe.wait_ge(s_exT, j + 1)
                    if known is None or known - 1 >= 2:
                        pe.wait_ge(s_eg, 2 * j - 2)
                    ex = expert_of[1]
                    for h in range(KT):
                        n = 0
                        for xp, wp in PARTS:
                            for kt in range(KT):
                                w = w12[:, bass.ds(ex, 1), 0, wp, kt, h * P:h * P + P].rearrange("p o n -> p (o n)")
                                last = mm(hps[2 * r + h][:, 0:TT], w, exT[:, r, (xp * KT + kt) * TT:(xp * KT + kt + 1) * TT],
                                          start=(n == 0), stop=(n == 3 * KT - 1))
                                n += 1
                        last.then_inc(s_ehp, 1)
                if live(known, 2, ET):
                    j, r = t - 2, (u - 2) % 2
                    ex = expert_of[2]
                    pe.wait_ge(s_elo, j + 1)
                    if known is None or known - 2 >= 2:
                        pe.wait_ge(s_ey, j - 1)
                    for s in range(2):
                        n = 0
                        for xp, wp in PARTS:
                            for kt in range(KT):
                                w = w12[:, bass.ds(ex, 1), 1, wp, kt, :].rearrange("p o n -> p (o n)")
                                last = mm(fold[r][:, s * H:s * H + H], ehl[:, r, xp, kt, s * P:s * P + P], w,
                                          start=(n == 0), stop=(n == 3 * KT - 1))
                                n += 1
                    last.then_inc(s_eyp, 1)

            pe.wait_ge(s_tab, 2)
            pe.wait_ge(s_el, 2 * E)
            steps(pe, expert_step, 1, ET + 2, ET)


_INS = ['x', 'adj', 'L0_gnn_W_self', 'L0_gnn_b_self', 'L0_gnn_W_nb', 'L0_gnn_b_nb', 'L0_gnn_W_comb', 'L0_gnn_b_comb',
        'L0_ffn_Wg', 'L0_ffn_bg', 'L0_ffn_W1', 'L0_ffn_b1', 'L0_ffn_W2', 'L0_ffn_b2']


def kernel(**inputs):
    import numpy as _np
    import concourse.bacc as _bacc
    from concourse import mybir as _mybir
    from concourse.bass_utils import run_bass_kernel_spmd as _run

    nc = _bacc.Bacc("TRN2", target_bir_lowering=False, num_devices=1)
    arrays, args = {}, []
    for name in _INS:
        a = _np.ascontiguousarray(inputs[name])
        arrays[f"in_{name}_dram"] = a
        args.append(nc.dram_tensor(f"in_{name}_dram", a.shape, _mybir.dt.from_np(a.dtype), kind="ExternalInput").ap())
    args.append(nc.dram_tensor("out_0_dram", inputs['x'].shape, _mybir.dt.float32, kind="ExternalOutput").ap())
    gnn_moe_kernel(nc, *args)
    r = _run(nc, [arrays], core_ids=[0])
    return r.results[0]["out_0_dram"]
```

```python
from contextlib import ExitStack

import concourse.bass as bass
from concourse import mybir

ALU = mybir.AluOpType
ACT = mybir.ActivationFunctionType
AX = mybir.AxisListType
F32 = mybir.dt.float32
F16 = mybir.dt.float16
F8 = mybir.dt.float8e4
I32 = mybir.dt.int32
U32 = mybir.dt.uint32
RED = bass.bass_isa.ReduceOp

P = 128
Q = 32
G = P // Q
EPS = 1e-5
XS = 2.0 ** 11


def gnn_moe_kernel(nc, x, adj, W_self, b_self, W_nb, b_nb, W_comb, b_comb, Wg, bg, W1, b1, W2, b2, out):
    N, D = x.shape
    E, _, H = W1.shape
    NT = N // P
    B = 4
    NG = NT // B
    KT = D // P
    NQ = N // G
    TT = 2 * P
    CAP = N + TT
    ET = -(-((2 * N + E * (TT - 1)) // TT) // B) * B
    DUM = ET - 2 * N // TT
    RW = 2 * D + 4
    assert D == H == 2 * P and N % (G * P) == 0 and E == 8 and B == 4

    xs_dram = nc.dram_tensor("dispatched", (E * CAP + DUM * TT, RW), F16, kind="Internal").ap()
    yp_dram = nc.dram_tensor("pair_out", (2 * N, D), F32, kind="Internal").ap()

    x_v = x.rearrange("(g k c e) d -> g k c (e d)", g=G, k=NG, c=Q, e=B)
    out_v = out.rearrange("(g k c e) d -> g k c (e d)", g=G, k=NG, c=Q, e=B)
    adj_v = adj.rearrange("(b k r e) (g j) -> k e g r b j", b=G, k=NG, r=Q, e=B, g=G)
    yp_v = yp_dram[0:2 * N, :].rearrange("(g k c e) d -> g k c (e d)", g=G, k=NG, c=Q, e=2 * B)

    with ExitStack() as ctx:
        def sb(name, shape, dt):
            return ctx.enter_context(nc.sbuf_tensor(name, shape, dt))

        def sem(name):
            return ctx.enter_context(nc.semaphore(name))

        bank = [ctx.enter_context(nc.psum_tensor(f"bank{i}", [P, 512], F32)) for i in range(8)]
        acc = bank[0:2]
        hps = bank[0:2] + bank[6:8]
        zbank = bank[0:2] + bank[4:6]
        tps = bank[2:4]
        fold = bank[4:6]
        wps = bank[6:8]
        cbank = bank[7]
        lbank, rbank, tbank = bank[4:6], bank[7], bank[6]

        x_sb = sb("x_sb", [P, NT, D], F32)
        rows = sb("rows", [P, NT * RW], F16)
        row16 = rows[:, :].rearrange("p (t d) -> p t d", t=NT)
        self_sb = rows[:, :].bitcast(F32).rearrange("p (t d) -> p t d", t=NT)
        row32 = rows[:, :].bitcast(I32).rearrange("p (t d) -> p t d", t=NT)
        z_flat = sb("z_flat", [P, NT * (D + 1)], F16)
        z_hi = z_flat[:, :].rearrange("p (t d) -> p t d", t=NT)
        z_lo = sb("z_lo", [P, NT, D], F16)
        stage = sb("stage", [P, 4, 2, NQ], I32)
        mask = sb("mask", [P, 2, G, NQ], F8)
        maskT = sb("maskT", [P, 4, G * NQ], F8)
        w12 = sb("w12", [P, E, 2, 2, KT, H], F16)
        wst = sb("wst", [P, 2, KT, H], F32)
        b1c = sb("b1c", [P, E, KT], F32)
        wg_f = sb("wg_f", [P, KT, E], F32)
        wg_s = sb("wg_s", [P, 2, KT, E], F16)
        bg_bc = sb("bg_bc", [P, E], F32)
        bc_bc = sb("bc_bc", [P, D], F32)
        const_bc = sb("const_bc", [P, D], F32)
        bcol = sb("bcol", [P, 2, KT], F32)
        diff = sb("diff", [P, P], I32)
        ident = sb("ident", [P, P], F16)
        identf = sb("identf", [P, P], F32)
        upper = sb("upper", [P, P], F16)
        ones = sb("ones", [P, P], F16)
        iota8 = sb("iota8", [P, E], F32)
        region = sb("region", [P, E], F32)
        mhalf = sb("mhalf", [P, B], F32)
        st6 = sb("st6", [P, 2, B, 6], F32)
        mv = sb("mv", [P, B, 2], F32)
        ve = sb("ve", [P, 2, NT], F32)
        rs = sb("rs", [P, 2, NT], F32)
        nbx = sb("nbx", [P, NT], F32)
        mv2 = sb("mv2", [P, B, 2], F32)
        xh = sb("xh", [P, 2, D], F32)
        xT = sb("xT", [P, 4, 4 * P], F16)
        sdeg = sb("sdeg", [P, 4], F32)
        rdeg = sb("rdeg", [P, 4], F32)
        tsum = sb("tsum", [P, 2, D], F32)
        lg = sb("lg", [P, B, E], F32)
        top = sb("top", [P, B, 8], F32)
        tidx = sb("tidx", [P, B, 8], U32)
        tidf = sb("tidf", [P, B, 2], F32)
        hot = sb("hot", [P, 2, B, E], F32)
        both = sb("both", [P, B, E], F16)
        base = sb("base", [P, B + 1, E], F16)
        m100 = sb("m100", [P, 1], F32)
        rk = sb("rk", [P, B, E], F32)
        pick = sb("pick", [P, 2, B, E], F32)
        slotf = sb("slotf", [P, 2, B], F32)
        slot = sb("slot", [P, NT, 2], I32)
        m12 = sb("m12", [P, NT, 2], F32)
        wdif = sb("wdif", [P, NT], F32)
        wexp = sb("wexp", [P, NT], F32)
        wden = sb("wden", [P, NT], F32)
        wts = sb("wts", [P, 2, NT], F32)
        fmx = sb("fmx", [P, 2], F32)
        fmr = sb("fmr", [P, 2], F32)
        fcl = sb("fcl", [P, 2], F32)
        fp2 = sb("fp2", [P, 2], F32)
        fin = sb("fin", [P, 2], F32)
        scw = sb("scw", [P, 5], F32)
        emx = sb("emx", [P, 3], F32)
        emr = sb("emr", [P, 3], F32)
        ecl = sb("ecl", [P, 3], F32)
        ep2 = sb("ep2", [P, 3], F32)
        ein = sb("ein", [P, 3], F32)
        s12 = sb("s12", [P, 2], F32)
        sc1 = sb("sc1", [P, E], F32)
        shs = sb("shs", [P, E], F32)
        sc2 = sb("sc2", [P, E], F32)
        tio = sb("tio", [P, ET], F32)
        q256 = sb("q256", [P, N // TT], F32)
        cntt = sb("cntt", [P, E], F32)
        nti = sb("nti", [P, E], F32)
        cinc = sb("cinc", [P, E], F32)
        coef = sb("coef", [P, E], F32)
        onesE = sb("onesE", [P, E], F32)
        texp = sb("texp", [P, ET], F32)
        tjmp = sb("tjmp", [P, ET], F32)
        padf = sb("padf", [P, E], F32)
        tab = sb("tab", [P, 2, ET], I32)
        padrow = sb("padrow", [P, E], I32)
        enum = sb("enum", [P, 4, 2], I32)
        pad = sb("pad", [P, 2, RW], F16)
        pad32 = pad[:, :, :].rearrange("p s n -> p (s n)").bitcast(I32).rearrange("p (s n) -> p s n", s=2)

        setup_mem = w12[:, :, :, :, :, :].rearrange("p e w q t n -> p (e w q t n)").bitcast(F32)
        cuts = [0, 0]

        def cut_setup(n):
            cuts[0] += n
            assert cuts[0] <= 2 * E * KT * H
            return setup_mem[:, cuts[0] - n:cuts[0]]

        wraw = cut_setup(4 * KT * D).rearrange("p (w t n) -> p w t n", w=4, t=KT)
        wT = cut_setup(2 * KT * D).rearrange("p (w t n) -> p w t n", w=2, t=KT)
        wsum = cut_setup(2 * KT * D).rearrange("p (t n) -> p t n", t=KT)
        bbig = cut_setup(2 * KT * P).rearrange("p (w t n) -> p w t n", w=2, t=KT)
        wf = cut_setup(2 * KT * D).bitcast(F16).rearrange("p (q t n) -> p q t n", q=2, t=KT)
        hl = cut_setup(4 * D).bitcast(F16).rearrange("p (a n) -> p a n", a=4)
        b2_bc = z_flat[:, :].bitcast(F32)[:, 0:E * H].rearrange("p (e n) -> p e n", e=E)

        ring = stage[:, :, :, :].rearrange("p a b c -> p (a b c)").bitcast(F32)

        def cut(n):
            cuts[1] += n
            assert cuts[1] <= 8 * NQ
            return ring[:, cuts[1] - n:cuts[1]]

        R = 4
        erow = cut(R * RW).bitcast(F16).rearrange("p (a s n) -> p a s n", a=R, s=2)
        erow32 = ring[:, 0:R * RW].bitcast(I32).rearrange("p (a s n) -> p a s n", a=R, s=2)
        ehid = cut(2 * TT * KT).rearrange("p (a t n) -> p a t n", a=2, t=KT)
        ehl = cut(2 * TT * KT).bitcast(F16).rearrange("p (a q t n) -> p a q t n", a=2, q=2, t=KT)
        exT = cut(2 * TT * KT).bitcast(F16).rearrange("p (a q n) -> p a (q n)", a=2, q=4)
        tge = cut(ET * E).rearrange("p (t e) -> p t e", t=ET)
        tgc = cut(ET * E).rearrange("p (t e) -> p t e", t=ET)
        cmpq = cut(E * N // TT).rearrange("p (e q) -> p e q", e=E)
        ysb = self_sb[:, 0:2 * R, 0:D].rearrange("p (a s) n -> p a s n", s=2)
        yin = [m.bitcast(F32).rearrange("p (a e k n) -> p a e k n", a=2, e=B, k=2)[:, a] for m in
               (z_lo[:, :, :].rearrange("p t n -> p (t n)"), maskT[:, :, :].rearrange("p a n -> p (a n)")) for a in range(2)]
        Y = len(yin)

        tp16 = [b_[:, 0:2 * P].bitcast(F16) for b_ in tps]
        etp16 = [b_[:, :].bitcast(F16) for b_ in tps]
        mask32 = [mask[:, i].rearrange("p b j -> p (b j)").bitcast(U32).rearrange("p (b k w) -> p b k w", b=G, k=NG) for i in range(2)]
        maskT32 = [maskT[:, i].bitcast(U32).rearrange("p (k b w) -> p b k w", b=G, k=NG) for i in range(4)]
        maskT8 = [maskT[:, i].rearrange("p (k m e) -> p k m e", k=NG, e=B) for i in range(4)]

        s_w, s_small, s_b12 = sem("weights_loaded"), sem("small_loaded"), sem("expert_biases_loaded")
        s_x = [sem("x0_loaded"), sem("x1_loaded"), sem("x2_loaded"), sem("x_rest_loaded")]
        s_iot, s_b2 = sem("table_iotas"), sem("b2_loaded")
        s_io, s_cst, s_idt, s_pad = sem("iotas"), sem("constants"), sem("identity"), sem("pad_rows")
        s_wtp, s_wtc, s_fold, s_wsum = sem("weights_transposed"), sem("wT_copied"), sem("weights_folded"), sem("fold_copied")
        s_fmx, s_fmr, s_fch, s_wf, s_bb, s_cp, s_cb = (sem(n) for n in (
            "fold_max", "fold_max_all", "fold_chain", "fold_split", "bias_spread", "const_product", "const_row"))
        s_st, s_ve, s_rs, s_nb = sem("stats_chain"), sem("variance"), sem("rstd"), sem("norm_scales")
        s_xh, s_hi, s_lo, s_tp, s_xT = sem("normalised"), sem("hi"), sem("lo"), sem("transposed"), sem("transposed_copied")
        s_zp, s_zhi, s_zlo = sem("setup_product"), sem("z_hi_made"), sem("z_lo_made")
        s_adj = [sem(f"adj_loaded{i}") for i in range(4)]
        s_mD, s_mA, s_T, s_mm = sem("mask_by_vector"), sem("mask_by_scalar"), sem("mask_transposed"), sem("neighbours_summed")
        s_dg, s_ts, s_x1, s_s2, s_ve2, s_rs2, s_rx2 = (sem(n) for n in (
            "degree_chain", "acc_read", "x1_made", "stats2_chain", "variance2", "rstd2", "scale2"))
        s_xh2, s_hi2, s_lo2, s_tp2, s_xT2, s_lgp = (sem(n) for n in (
            "normalised2", "hi2", "lo2", "transposed2", "transposed2_copied", "logits_product"))
        s_lg = sem("logits")
        s_rc, s_both, s_sl, s_rkp, s_slot = (sem(n) for n in ("route_chain", "one_hots", "slot_chain", "ranks", "slots"))
        s_sc = sem("dispatched")
        s_ew, s_emx, s_emr, s_ech, s_es, s_eh, s_el = (sem(n) for n in (
            "expert_weights_loaded", "expert_max", "expert_max_all", "expert_chain", "expert_scales",
            "expert_hi", "expert_lo"))
        s_tot, s_tch, s_tab, s_padw, s_dum = (sem(n) for n in (
            "totals", "table_chain", "tables", "pads_written", "dummies_written"))
        s_wd, s_wx, s_wc, s_wm = sem("logit_gap"), sem("gap_exp"), sem("mix_chain"), sem("mix_weights")
        s_er = [sem(f"expert_rows_loaded{i}") for i in range(R)]
        s_etp, s_idc, s_exT, s_ehp, s_eg, s_ehi, s_elo, s_eyp, s_ey = (sem(n) for n in (
            "e_transposed", "e_numbers_copied", "e_transposed_copied", "e_hidden_product", "e_hidden", "e_hidden_hi", "e_hidden_lo",
            "e_out_product", "e_out"))
        s_ysc = [sem(f"outputs_scattered{i}") for i in range(R)]
        s_yl, s_o1, s_o2, s_out = [sem(f"pairs_loaded{i}") for i in range(Y)], sem("first_added"), sem("second_added"), sem("out_written")

        class Chain:

            def __init__(self, eng, s, base):
                self.eng, self.s, self.base, self.n = eng, s, base, 0

            def __call__(self, ins):
                self.n += 1
                ins.then_inc(self.s, 1)
                self.eng.wait_ge(self.s, self.base + self.n)

        def flat(a, t):
            return a[:, at(t), :].rearrange("p o n -> p (o n)")

        def spread(a, n=B):
            return a[:, :].rearrange("p (o e) -> p o e", o=1).to_broadcast((P, n, E))

        def at(t, n=1):
            return slice(t, t + n) if isinstance(t, int) else bass.ds(t, n)

        def div(t, u, known, lag, n):
            return (known - lag) // n if known is not None else (B // n) * kreg[0] + (u - lag) // n

        kreg = [None]

        X1, NORM, LOGIT, SCORE, HOT, SLOT = 3, 4, 5,7,10,12
        PT, PL, PR = 3,4,9
        EMAX, ESCALE, ESPLIT = 1, 2, 3
        GATE_STEPS = NT + SLOT - B + 1

        def steps(eng, step, peel, end, total=None, tail=0):
            total = NT if total is None else total
            for t in range(B * peel):
                step(t, t, t)
            with eng.Fori(peel, total // B - tail) as k:
                kreg[0] = k
                for e in range(B):
                    step(B * k + e, e, None)
            for t in range(total - B * tail, end):
                step(t, t, t)

        def live(known, lag, total=None):
            total = NT if total is None else total
            return known is None or 0 <= known - lag < total

        def write_pads(eng, experts):
            eng.wait_ge(s_pad, 2)
            eng.wait_ge(s_tab, 2)
            for e in experts:
                row = eng.value_load(padrow[0:1, e:e + 1], min_val=0, max_val=E * CAP - TT)
                eng.dma_start(xs_dram[bass.ds(row, TT), :].rearrange("(p s) n -> p (s n)", s=2),
                              pad[:, :, :].rearrange("p s n -> p (s n)")).then_inc(s_padw, 16)

        def load_experts(eng, held, lags, t, u, known):
            kept = {j: r for j, r in held.get("tiles", {}).items() if u > 0}
            held["tiles"] = {}
            for lag in lags:
                if live(known, lag, ET):
                    held[lag] = kept.get(u - lag)
                    if held[lag] is None:
                        held[lag] = eng.value_load(tab[0:1, 1, at(t - lag)], min_val=0, max_val=E - 1)
                    kept[u - lag] = held[lag]
            held["tiles"] = {j: r for j, r in kept.items() if j > u - max(lags)}

        def apart(eng):
            eng.nop(nofuse=True)

        block = ctx.enter_context(nc.Block())

        @block.sync
        def _(sp):
            def load_x(k, s):
                for g in range(G):
                    sp.dma_start(x_sb[Q * g:Q * g + Q, B * k:B * k + B, :].rearrange("p e d -> p (e d)"),
                                 x_v[g, k]).then_inc(s, 16)

            for k in range(NG):
                load_x(k, s_x[min(k, 3)])

            def load_adj(t, u, known):
                for h in range(2):
                    s = 2 * (u % 2) + h
                    if known is None or known >= 2:
                        sp.wait_ge((s_mD, s_mA)[h], t - 1)
                    for g in range(G):
                        if known is not None:
                            src = adj_v[t // B, t % B, g]
                        else:
                            src = adj_v[bass.ds(kreg[0], 1), u, g].rearrange("o r b j -> (o r) b j")
                        sp.dma_start(stage[Q * g:Q * g + Q, s], src[:, 2 * h:2 * h + 2, :]).then_inc(s_adj[s], 16)

            steps(sp, load_adj, 1, NT)

            sp.wait_ge(s_mm, NT)
            sp.dma_start(b2_bc[:, :, :].rearrange("p e n -> p (e n)"),
                         b2.rearrange("(o e) n -> o (e n)", o=1).to_broadcast((P, E * H))).then_inc(s_b2, 16)
            write_pads(sp, range(0, E, 2))
            sp.wait_ge(s_padw, 16 * E)
            sp.wait_ge(s_dum, 16 * DUM)
            sp.wait_ge(s_sc, 16 * 2 * NT)

            def load_rows(t, u, known):
                a = u % R
                if known is None or known >= R:
                    sp.wait_ge(s_etp, t - R + 1)
                    sp.wait_ge(s_idc, t - R + 1)
                    apart(sp)
                row = sp.value_load(tab[0:1, 0, at(t)], min_val=0, max_val=E * CAP + (DUM - 1) * TT)
                sp.dma_start(erow[:, a], xs_dram[bass.ds(row, TT), :].rearrange("(p s) n -> p s n", s=2)).then_inc(s_er[a], 16)

            steps(sp, load_rows, 1, ET, ET)

            for a in range(R):
                sp.wait_ge(s_ysc[a], 32 * (ET // R))
            def load_pairs(k, par, first):
                if not first:
                    sp.wait_ge(s_o2, B * (k - Y + 1))
                    apart(sp)
                for g in range(G):
                    src = yp_v[g, k] if first else yp_v[g, at(k)].rearrange("o c n -> (o c) n")
                    sp.dma_start(yin[par][Q * g:Q * g + Q].rearrange("p e k n -> p (e k n)"), src).then_inc(s_yl[par], 16)

            for k in range(Y):
                load_pairs(k, k, True)
            with sp.Fori(1, NG // Y) as kk:
                for par in range(Y):
                    load_pairs(Y * kk + par, par, False)
            sp.wait_ge(s_out, 16 * G * NG)

        @block.gpsimd
        def _(pool):
            gp = nc.gpsimd
            gp.iota(diff[:, :], [[1, P]], base=0, channel_multiplier=-1).then_inc(s_io, 1)
            gp.memset(mhalf[:, :], -0.5).then_inc(s_io, 1)
            small = dict(channel_multiplier=0, allow_small_or_imprecise_dtypes=True)
            gp.iota(iota8[:, :], [[1, E]], base=0, **small).then_inc(s_io, 1)
            gp.iota(region[:, :], [[CAP, E]], base=0, **small).then_inc(s_io, 1)
            gp.iota(q256[:, :], [[TT, N // TT]], base=0, **small).then_inc(s_iot, 1)
            gp.iota(tio[:, :], [[1, ET]], base=0, **small).then_inc(s_iot, 1)
            for g in range(G):
                pool.wait_ge(s_io, 4 + g)
                gp.iota(row32[Q * g:Q * g + Q, :, D:D + 1], [[2 * P, NG], [2, B], [0, 1]], base=2 * NQ * g,
                        channel_multiplier=2 * B).then_inc(s_io, 1)
            pool.wait_ge(s_io, 8)
            gp.memset(pad[:, :, :], 0.0).then_inc(s_pad, 1)
            pool.wait_ge(s_pad, 1)
            gp.iota(pad32[:, :, D:D + 1], [[1, 2], [0, 1]], base=2 * N, channel_multiplier=2).then_inc(s_pad, 1)

            def rstd(k):
                pool.wait_ge(s_ve, k + 1)
                gp.tensor_tensor(rs[:, 0, at(B * k, B)], ve[:, 0, at(B * k, B)], mhalf[:, :], ALU.pow).then_inc(s_rs, 1)

            rstd(0)
            pool.wait_ge(s_fmx, 2)
            gp.partition_all_reduce(fmr[:, :], fmx[:, :], P, RED.absmax).then_inc(s_fmr, 1)
            rstd(1)

            def expert_load(k):
                if k:
                    pool.wait_ge(s_el, 2 * k)
                for w, m in enumerate((W1, W2)):
                    pool.dma_start(wst[:, w], m[k].rearrange("(t p) n -> p t n", p=P)).then_inc(s_ew, 16)

            def expert_max(k):
                pool.wait_ge(s_emx, k + 1)
                gp.partition_all_reduce(emr[:, :], emx[:, :], P, RED.absmax).then_inc(s_emr, 1)

            def dispatch(t):
                pool.wait_ge(s_lo2, t + 1)
                pool.wait_ge(s_hi2, t + 1)
                pool.wait_ge(s_slot, t // B + 1)
                for c in range(2):
                    gp.indirect_dma_start(
                        out=xs_dram[:, :], out_offset=bass.IndirectOffsetOnAxis(ap=slot[:, t, c:c + 1], axis=0),
                        in_=self_sb[:, t, :].bitcast(F16), in_offset=None).then_inc(s_sc, 16)


            def setup_step(t, u, known):
                if u % B == 1 and (known is None or known + 2 * B - 1 < NT):
                    rstd(div(t, u, known, 1, B) + 2)
                pool.wait_ge(s_hi, t + 1)
                apart(pool)
                gp.tensor_tensor(hl[:, u % 4, D:2 * D], xh[:, u % 2, :], hl[:, u % 4, 0:D], ALU.subtract).then_inc(s_lo, 1)

            steps(pool, setup_step, 1, NT, tail=2)
            pool.dma_start(b1c[:, :, :], b1.rearrange("e (t p) -> p e t", p=P), allow_slow_non_contiguous=True).then_inc(s_b12, 16)
            expert_load(0)
            pool.wait_ge(s_pad, 2)
            for q in range(DUM):
                pool.dma_start(xs_dram[E * CAP + q * TT:E * CAP + (q + 1) * TT, :].rearrange("(p s) n -> p (s n)", s=2),
                               pad[:, :, :].rearrange("p s n -> p (s n)")).then_inc(s_dum, 16)
            sent = 0
            for s in range(GATE_STEPS + 1):
                if 0 <= s - X1 < NT:
                    t = s - X1
                    pool.wait_ge(s_ve2, t + 1)
                    gp.tensor_tensor(rs[:, 1, t:t + 1], ve[:, 1, t:t + 1], mhalf[:, 0:1], ALU.pow).then_inc(s_rs2, 1)
                if 0 <= s - EMAX < NT and (s - EMAX) % B == 0:
                    expert_max((s - EMAX) // B)
                if 0 <= s - ESPLIT - 1 < NT - B and (s - ESPLIT - 1) % B == 0:
                    expert_load((s - ESPLIT - 1) // B + 1)
                for _ in range(1 if s < NT-2 else 2):
                    if sent < B * ((s - SLOT) // B + 1):
                        dispatch(sent)
                        sent += 1

            def scatter(t, u, known):
                a = u % R
                pool.wait_ge(s_idc, t + 1)
                pool.wait_ge(s_ey, t + 1)
                apart(pool)
                for s in range(2):
                    gp.indirect_dma_start(
                        out=yp_dram[:, :], out_offset=bass.IndirectOffsetOnAxis(ap=enum[:, a, s:s + 1], axis=0),
                        in_=ysb[:, a, s, :], in_offset=None, bounds_check=2 * N - 1, oob_is_err=False).then_inc(s_ysc[a], 16)

            steps(pool, scatter, 1, ET, ET)

        @block.scalar
        def _(act):
            sc = nc.scalar
            for w, m in enumerate((W_self, W_nb)):
                act.dma_start(wraw[:, w], m.rearrange("(t p) n -> p t n", p=P)).then_inc(s_w, 16)
            act.dma_start(wraw[:, 2:4].rearrange("p w t n -> p (w t) n"),
                          W_comb.rearrange("(t p) n -> p t n", p=P)).then_inc(s_w, 16)
            act.dma_start(bcol[:, 0, :], b_self.rearrange("(t p) -> p t", p=P), allow_slow_non_contiguous=True).then_inc(s_small, 16)
            act.dma_start(bcol[:, 1, :], b_nb.rearrange("(t p) -> p t", p=P), allow_slow_non_contiguous=True).then_inc(s_small, 16)
            act.dma_start(wg_f[:, :, :], Wg.rearrange("(t p) n -> p t n", p=P)).then_inc(s_small, 16)
            act.dma_start(bc_bc[:, :], b_comb.rearrange("(o n) -> o n", o=1).to_broadcast((P, D))).then_inc(s_small, 16)
            act.dma_start(bg_bc[:, :], bg.rearrange("(o n) -> o n", o=1).to_broadcast((P, E))).then_inc(s_small, 16)

            def setup_step(t, u, known):
                if live(known, 0):
                    if known is None or known >= 2:
                        act.wait_ge(s_lo, t - 1)
                    act.wait_ge(s_nb, div(t, u, known, 0, B) + 1)
                    sc.activation(xh[:, u % 2, :], flat(x_sb, t), ACT.Identity, bias=nbx[:, at(t)],
                                  scale=rs[:, 0, at(t)]).then_inc(s_xh, 1)
                    if known is None or known >= 4:
                        act.wait_ge(s_tp, t - 3)
                    act.wait_ge(s_xh, t + 1)
                    sc.copy(hl[:, u % 4, 0:D], xh[:, u % 2, :]).then_inc(s_hi, 1)
                if live(known, 2):
                    act.wait_ge(s_tp, t - 1)
                    if known is None or known >= 6:
                        act.wait_ge(s_zp, t - 5)
                    sc.copy(xT[:, (u - 2) % 4, :], tp16[(u - 2) % 2]).then_inc(s_xT, 1)

                if known in AHEAD:
                    i = AHEAD.index(known)
                    masks(i, i, i)

            AHEAD = (NT - 2, NT)

            def masks(t, u, known):
                s = 2 * (u % 2) + 1
                act.wait_ge(s_adj[s], 64 * (div(t, u, known, 0, 2) + 1))
                if known is None or known >= 2:
                    act.wait_ge(s_T, t - 1)
                apart(act)
                sc.activation(mask[:, u % 2, 2:4, :], stage[:, s], ACT.Sigmoid, bias=m100[:, 0:1], scale=200.0,
                              saturate=False).then_inc(s_mA, 1)

            act.wait_ge(s_cst, 1)
            steps(act, setup_step, 2, NT + 4, tail=2)

            def main_step(t, u, known):
                if live(known, 0) and known not in (0, 1):
                    masks(t, u, known)
                if live(known, NORM):
                    act.wait_ge(s_xh2, t - NORM + 1)
                    sc.copy(row16[:, at(t - NORM), 0:D].rearrange("p o d -> p (o d)"), xh[:, (u - NORM) % 2, :]).then_inc(s_hi2, 1)
                if live(known, LOGIT):
                    act.wait_ge(s_tp2, t - LOGIT + 1)
                    if known is None or known - LOGIT >= 4:
                        act.wait_ge(s_lgp, t - LOGIT - 3)
                    sc.copy(xT[:, (u - LOGIT) % 4, :], tps[(u - LOGIT) % 2][:, :]).then_inc(s_xT2, 1)
                if u % B == ESPLIT % B and live(known, ESPLIT):
                    expert_hi(div(t, u, known, ESPLIT, B))

            def expert_hi(k):
                act.wait_ge(s_es, k + 1)
                for w in range(2):
                    sc.activation(w12[:, at(k), w, 0].rearrange("p o t n -> p (o t n)"), wst[:, w].rearrange("p t n -> p (t n)"),
                                  ACT.Copy, scale=s12[:, w:w + 1]).then_inc(s_eh, 1)

            act.wait_ge(s_zp, NT)
            steps(act, main_step, 3, NT + LOGIT)

            write_pads(act, range(1, E, 2))
            act.wait_ge(s_wd, 1)
            sc.activation(wexp[:, :], wdif[:, :], ACT.Exp).then_inc(s_wx, 1)

            def expert_step(t, u, known):
                ex = act.value_load(tab[0:1, 1, at(t)], min_val=0, max_val=E - 1)
                if known is None or known >= 2:
                    act.wait_ge(s_elo, t - 1)
                for h in range(KT):
                    act.wait_ge(s_ehp, 2 * t + h + 1)
                    sc.activation(ehid[:, u % 2, h, :], hps[2 * (u % 2) + h][:, 0:TT], ACT.Gelu,
                                  bias=b1c[:, bass.ds(ex, 1), h], scale=sc1[:, bass.ds(ex, 1)]).then_inc(s_eg, 1)
                act.wait_ge(s_eg, 2 * t + 2)
                if known is None or known >= 2:
                    act.wait_ge(s_eyp, t - 1)
                sc.activation(ehl[:, u % 2, 0].rearrange("p t n -> p (t n)"), ehid[:, u % 2].rearrange("p t n -> p (t n)"),
                              ACT.Copy, scale=shs[:, bass.ds(ex, 1)]).then_inc(s_ehi, 1)

            act.wait_ge(s_tab, 2)
            act.wait_ge(s_b12, 16)
            steps(act, expert_step, 1, ET, ET)

            with act.Fori(0, NG) as k:
                act.wait_ge(s_o2, B * k + B)
                for g in range(G):
                    act.dma_start(out_v[g, bass.ds(k, 1)].rearrange("o c n -> (o c) n"),
                                  x_sb[Q * g:Q * g + Q, bass.ds(B * k, B), :].rearrange("p e d -> p (e d)")).then_inc(s_out, 16)

        @block.vector
        def _(dve):
            v = nc.vector

            def stats_a(k):
                for e in range(B):
                    v.bn_stats(st6[:, 0, e, :], flat(x_sb, B * k + e)).then_inc(s_st, 1)
                dve.wait_ge(s_st, 2 * B * k + B)
                for e in range(B):
                    if e == 0:
                        apart(dve)
                    v.bn_aggr(mv[:, e, :], st6[:, 0, e, :]).then_inc(s_st, 1)
                dve.wait_ge(s_st, 2 * B * (k + 1))
                v.tensor_scalar(ve[:, 0, at(B * k, B)], mv[:, :, 1],
                                EPS, XS ** -2, ALU.add, ALU.mult).then_inc(s_ve, 1)

            def stats_b(k):
                dve.wait_ge(s_rs, k + 1)
                v.scalar_tensor_tensor(nbx[:, at(B * k, B)], mv[:, :, 0],
                                       -1.0, rs[:, 0, at(B * k, B)], ALU.mult, ALU.mult).then_inc(s_nb, 1)

            def powers(ch, out_, inv, mx):
                ch(v.tensor_scalar(mx, mx, 1e-30, None, ALU.max))
                ch(v.tensor_scalar(out_.bitcast(U32), mx.bitcast(U32), 0x7F800000, None, ALU.bitwise_and))
                ch(v.reciprocal(inv, out_))

            dve.wait_ge(s_io, 8)
            v.tensor_scalar(identf[:, :], diff[:, :], 0.0, None, ALU.is_equal).then_inc(s_idt, 1)
            v.tensor_scalar(ident[:, :], diff[:, :], 0.0, None, ALU.is_equal).then_inc(s_idt, 1)
            v.tensor_scalar(upper[:, :], diff[:, :], 0.0, None, ALU.is_gt).then_inc(s_idt, 1)
            v.memset(ones[:, :], 1.0).then_inc(s_idt, 1)
            v.memset(m100[:, :], -100.0).then_inc(s_cst, 1)
            v.memset(onesE[:, :], 1.0).then_inc(s_cst, 1)
            v.memset(z_hi[:, :, D:D + 1], 1.0).then_inc(s_cst, 1)
            v.memset(base[:, :, :], 0.0).then_inc(s_cst, 1)
            dve.wait_ge(s_x[0], 16 * G)
            stats_a(0)

            for w in range(2):
                dve.wait_ge(s_wtp, w + 1)
                v.tensor_copy(wT[:, w].rearrange("p t n -> p (t n)"), wps[w][:, :]).then_inc(s_wtc, 1)
            dve.wait_ge(s_small, 16 * 5)
            dve.wait_ge(s_idt, 4)
            for w in range(2):
                for t in range(KT):
                    v.tensor_scalar(bbig[:, w, t, :], ones[:, :], bcol[:, w, t:t + 1], None, ALU.mult).then_inc(s_bb, 1)
            stats_b(0)
            dve.wait_ge(s_fold, 1)
            for t in range(KT):
                v.tensor_copy(wsum[:, t, :], fold[t][:, :]).then_inc(s_wsum, 1)
            dve.wait_ge(s_wsum, KT)
            v.tensor_reduce(fmx[:, 0:1], wsum[:, :, :].rearrange("p t n -> p (t n)"), AX.X, ALU.max, apply_absolute_value=True).then_inc(s_fmx, 1)
            v.tensor_reduce(fmx[:, 1:2], wg_f[:, :, :].rearrange("p t n -> p (t n)"), AX.X, ALU.max, apply_absolute_value=True).then_inc(s_fmx, 1)
            dve.wait_ge(s_cp, 1)
            v.tensor_tensor(const_bc[:, :], cbank[:, 0:D], bc_bc[:, :], ALU.add).then_inc(s_cb, 1)
            dve.wait_ge(s_x[1], 16 * G)
            stats_a(1)
            dve.wait_ge(s_fmr, 1)
            ch = Chain(dve, s_fch, 0)
            powers(ch, fp2[:, :], fin[:, :], fmr[:, :])
            ch(v.tensor_scalar(scw[:, 0:2], fin[:, :], 2.0 ** 14, None, ALU.mult))
            ch(v.tensor_scalar(scw[:, 2:4], fp2[:, :], 2.0 ** -14 / XS, None, ALU.mult))
            ch(v.tensor_scalar(scw[:, 4:5], fin[:, 0:1], 2.0 ** 6, None, ALU.mult))
            for out_, in_, c in ((wf, wsum, 0), (wg_s, wg_f, 1)):
                v.tensor_scalar(out_[:, 0], in_[:, :, :], scw[:, c:c + 1], None, ALU.mult).then_inc(s_wf, 1)
                dve.wait_ge(s_wf, 2 * c + 1)
                v.scalar_tensor_tensor(out_[:, 1], in_[:, :, :], scw[:, c:c + 1], out_[:, 0], ALU.mult, ALU.subtract).then_inc(s_wf, 1)

            def setup_step(t, u, known):
                nxt = div(t, u, known, 0, B) + 2
                if u % B == 0 and (known is None or known + 2 * B < NT):
                    if known == 0:
                        dve.wait_ge(s_x[2], 16 * G)
                    else:
                        dve.wait_ge(s_x[3], 16 * G * (NG - 3))
                    stats_a(nxt)
                if live(known, 5):
                    b_ = zbank[(u - 5) % 4]
                    dve.wait_ge(s_zp, t - 4)
                    v.tensor_scalar(z_hi[:, at(t - 5), 0:D].rearrange("p o d -> p (o d)"), b_[:, D:2 * D],
                                    2.0 ** -19, None, ALU.mult).then_inc(s_zhi, 1)
                    v.scalar_tensor_tensor(self_sb[:, at(t - 5), 0:D].rearrange("p o d -> p (o d)"), b_[:, 0:D],
                                           scw[:, 2:3], const_bc[:, :], ALU.mult, ALU.add)
                    dve.wait_ge(s_zhi, t - 4)
                    v.scalar_tensor_tensor(flat(z_lo, t - 5), b_[:, D:2 * D], 2.0 ** -19,
                                           z_hi[:, at(t - 5), 0:D].rearrange("p o d -> p (o d)"),
                                           ALU.mult, ALU.subtract).then_inc(s_zlo, 1)
                if u % B == 2 and (known is None or known + 2 * B - 2 < NT):
                    stats_b(nxt)
                if known in AHEAD:
                    i = AHEAD.index(known)
                    masks(i, i, i)
                if known in AHEAD_T:
                    i = AHEAD_T.index(known)
                    mask_transpose(i, i, i)

            AHEAD, AHEAD_T = (NT - 2, NT), (NT + 1, NT + 3)

            def masks(t, u, known):
                s = 2 * (u % 2)
                if known is None or known >= 2:
                    dve.wait_ge(s_T, t - 1)
                dve.wait_ge(s_adj[s], 64 * (div(t, u, known, 0, 2) + 1))
                apart(dve)
                v.tensor_scalar(mask[:, u % 2, 0:2, :], stage[:, s], 0.0, None, ALU.is_gt, saturate=False).then_inc(s_mD, 1)

            def mask_transpose(t, u, known):
                dve.wait_ge(s_mD, t + 1)
                dve.wait_ge(s_mA, t + 1)
                if known is None or known >= 4:
                    dve.wait_ge(s_mm, t - 3)
                v.transpose(maskT32[u % 4], mask32[u % 2]).then_inc(s_T, 1)

            stats_b(1)
            dve.wait_ge(s_cb, 1)
            steps(dve, setup_step, 2, NT + 5, tail=2)

            def main_step(t, u, known):
                if live(known, NORM):
                    j = t - NORM
                    dve.wait_ge(s_rs2, j + 1)
                    if known is None or known - NORM >= 2:
                        dve.wait_ge(s_hi2, j - 1)
                    v.tensor_scalar(xh[:, (u - NORM) % 2, :], flat(x_sb, j), mv2[:, (u - NORM) % 4, 0:1], rs[:, 1, at(j)],
                                    ALU.subtract, ALU.mult).then_inc(s_xh2, 1)
                if live(known, X1):
                    j, p, r = t - X1, acc[(u - X1) % 2], (u - X1) % 4
                    dve.wait_ge(s_mm, j + 1)
                    v.tensor_scalar(sdeg[:, r:r + 1], p[:, D:D + 1], 1.0, scw[:, 4:5], ALU.max, ALU.mult).then_inc(s_dg, 1)
                if live(known, 0) and known not in (0, 1):
                    masks(t, u, known)
                if live(known, X1):
                    dve.wait_ge(s_dg, 2 * j + 1)
                    v.reciprocal(rdeg[:, r:r + 1], sdeg[:, r:r + 1]).then_inc(s_dg, 1)
                    dve.wait_ge(s_dg, 2 * j + 2)
                    v.scalar_tensor_tensor(tsum[:, r % 2, :], p[:, 0:D], rdeg[:, r:r + 1],
                                           self_sb[:, at(j), 0:D].rearrange("p o d -> p (o d)"), ALU.mult, ALU.add).then_inc(s_ts, 1)
                if live(known, NORM):
                    i = t - NORM
                    dve.wait_ge(s_hi2, i + 1)
                    v.tensor_tensor(row16[:, at(i), D:2 * D].rearrange("p o d -> p (o d)"), xh[:, (u - NORM) % 2, :],
                                    row16[:, at(i), 0:D].rearrange("p o d -> p (o d)"), ALU.subtract).then_inc(s_lo2, 1)
                if live(known, X1):
                    dve.wait_ge(s_ts, j + 1)
                    v.scalar_tensor_tensor(flat(x_sb, j), tsum[:, r % 2, :], 0.0, flat(x_sb, j), ALU.max, ALU.add).then_inc(s_x1, 1)
                if live(known, 0) and known not in (0, 1):
                    mask_transpose(t, u, known)
                if live(known, X1):
                    dve.wait_ge(s_x1, j + 1)
                    apart(dve)
                    v.bn_stats(st6[:, 1, r, :], flat(x_sb, j)).then_inc(s_s2, 1)
                    dve.wait_ge(s_s2, 2 * j + 1)
                    apart(dve)
                    v.bn_aggr(mv2[:, r, :], st6[:, 1, r, :]).then_inc(s_s2, 1)
                    dve.wait_ge(s_s2, 2 * j + 2)
                    v.tensor_scalar(ve[:, 1, at(j)], mv2[:, r, 1:2], EPS, XS ** -2, ALU.add, ALU.mult).then_inc(s_ve2, 1)
                if u % B == EMAX % B and live(known, EMAX):
                    expert_max(div(t, u, known, EMAX, B))
                if u % B == ESCALE % B and live(known, ESCALE):
                    expert_scales(div(t, u, known, ESCALE, B))
                if u % B == ESPLIT % B and live(known, ESPLIT):
                    expert_lo(div(t, u, known, ESPLIT, B))
                if live(known, SCORE):
                    i = t - SCORE
                    dve.wait_ge(s_lgp, i + 1)
                    v.scalar_tensor_tensor(lg[:, (u - SCORE) % B, :], lbank[(u - SCORE) % 2][:, 0:E], scw[:, 3:4], bg_bc[:, :],
                                           ALU.mult, ALU.add).then_inc(s_lg, 1)
                if u % B == HOT % B and live(known, HOT):
                    choose(div(t, u, known, HOT, B))
                if u % B == SLOT % B and live(known, SLOT):
                    slots(div(t, u, known, SLOT, B))

            def expert_max(k):
                dve.wait_ge(s_ew, 32 * (k + 1))
                dve.wait_ge(s_b12, 16)
                for w in range(2):
                    v.tensor_reduce(emx[:, w:w + 1], wst[:, w].rearrange("p t n -> p (t n)"), AX.X, ALU.max, apply_absolute_value=True)
                v.tensor_reduce(emx[:, 2:3], flat(b1c, k), AX.X, ALU.max, apply_absolute_value=True).then_inc(s_emx, 1)

            def expert_scales(k):
                dve.wait_ge(s_emr, k + 1)
                ch = Chain(dve, s_ech, 4 * k)
                v.tensor_copy(ecl[:, 0:2], emr[:, 0:2])
                ch(v.scalar_tensor_tensor(ecl[:, 2:3], emr[:, 0:1], float(D), emr[:, 2:3], ALU.mult, ALU.add))
                powers(ch, ep2[:, :], ein[:, :], ecl[:, :])
                v.tensor_scalar(sc1[:, at(k)], ep2[:, 0:1], 2.0 ** -14 / XS, None, ALU.mult)
                v.tensor_scalar(shs[:, at(k)], ein[:, 2:3], 2.0 ** 14, None, ALU.mult)
                v.scalar_tensor_tensor(sc2[:, at(k)], ep2[:, 2:3], 2.0 ** -28, ep2[:, 1:2], ALU.mult, ALU.mult)
                v.tensor_scalar(s12[:, :], ein[:, 0:2], 2.0 ** 14, None, ALU.mult).then_inc(s_es, 1)

            def expert_lo(k):
                dve.wait_ge(s_eh, 2 * k + 2)
                for w in range(2):
                    v.scalar_tensor_tensor(w12[:, at(k), w, 1].rearrange("p o t n -> p (o t n)"),
                                           wst[:, w].rearrange("p t n -> p (t n)"), s12[:, w:w + 1],
                                           w12[:, at(k), w, 0].rearrange("p o t n -> p (o t n)"),
                                           ALU.mult, ALU.subtract).then_inc(s_el, 1)

            def choose(k):
                dve.wait_ge(s_lg, B * (k + 1))
                if not isinstance(k, int) or k:
                    dve.wait_ge(s_both, k)
                ch = Chain(dve, s_rc, HN * k)
                apart(dve)
                for b_ in range(B):
                    last = v.max(top[:, b_, :], lg[:, b_, :])
                ch(last)
                v.tensor_copy(m12[:, at(B * k, B), :], top[:, :, 0:2])
                for b_ in range(B):
                    last = v.max_index(tidx[:, b_, :], top[:, b_, :], lg[:, b_, :])
                ch(last)
                ch(v.tensor_copy(tidf[:, :, :], tidx[:, :, 0:2]))
                v.tensor_copy(row32[:, at(B * k, B), D + 1:D + 2], tidf[:, :, 0:1])
                for c in range(2):
                    last = v.tensor_tensor(hot[:, c], spread(iota8), tidf[:, :, c:c + 1].to_broadcast((P, B, E)), ALU.is_equal)
                ch(last)
                ch(v.tensor_tensor(both[:, :, :], hot[:, 0], hot[:, 1], ALU.add))
                ch(v.tensor_copy(base[:, 0, :], base[:, B, :]))
                for b_ in range(B - 1):
                    ch(v.tensor_tensor(base[:, b_ + 1, :], base[:, b_, :], both[:, b_, :], ALU.add))
                v.tensor_tensor(base[:, B, :], base[:, B - 1, :], both[:, B - 1, :], ALU.add).then_inc(s_both, 1)
                assert ch.n == HN

            HN = 6 + B - 1

            def slots(k):
                dve.wait_ge(s_rkp, k + 1)
                ch = Chain(dve, s_sl, 3 * k)
                ch(v.tensor_tensor(rk[:, :, :], rbank[:, 0:B * E].rearrange("p (b e) -> p b e", b=B), spread(region), ALU.add))
                for c in range(2):
                    last = v.tensor_tensor(pick[:, c], hot[:, c], rk[:, :, :], ALU.mult)
                ch(last)
                ch(v.tensor_reduce(slotf[:, :, :], pick[:, :, :, :], AX.X, ALU.add))
                v.tensor_copy(slot[:, at(B * k, B), :].rearrange("p t c -> p c t"), slotf[:, :, :]).then_inc(s_slot, 1)

            steps(dve, main_step, 4, GATE_STEPS + 1)

            dve.wait_ge(s_tot, 1)
            dve.wait_ge(s_iot, 2)
            ch = Chain(dve, s_tch, 0)
            ch(v.tensor_copy(cntt[:, :], tbank[:, 0:E]))
            ch(v.tensor_tensor(cmpq[:, :, :], cntt[:, :].rearrange("p (e o) -> p e o", o=1).to_broadcast((P, E, N // TT)),
                               q256[:, :].rearrange("p (o q) -> p o q", o=1).to_broadcast((P, E, N // TT)), ALU.is_gt))
            ch(v.tensor_reduce(nti[:, :], cmpq[:, :, :], AX.X, ALU.add))
            ch(v.tensor_tensor_scan(cinc[:, :], onesE[:, :], nti[:, :], 0.0, ALU.mult, ALU.add))
            ch(v.tensor_scalar(coef[:, :], nti[:, :], -float(TT), float(CAP), ALU.mult, ALU.add))
            ch(v.tensor_tensor(tge[:, :, :], tio[:, :].rearrange("p (t o) -> p t o", o=1).to_broadcast((P, ET, E)), spread(cinc, ET), ALU.is_ge))
            ch(v.tensor_tensor(tgc[:, :, :], tge[:, :, :], spread(coef, ET), ALU.mult))
            ch(v.tensor_reduce(tjmp[:, :], tgc[:, :, :], AX.X, ALU.add))
            ch(v.tensor_reduce(texp[:, :], tge[:, :, :], AX.X, ALU.add))
            v.scalar_tensor_tensor(tab[:, 0, :], tio[:, :], float(TT), tjmp[:, :], ALU.mult, ALU.add)
            v.tensor_scalar(tab[:, 1, :], texp[:, :], float(E - 1), None, ALU.min).then_inc(s_tab, 1)
            v.tensor_tensor(padrow[:, :], cntt[:, :], region[:, :], ALU.add).then_inc(s_tab, 1)
            v.tensor_tensor(wdif[:, :], m12[:, :, 1], m12[:, :, 0], ALU.subtract).then_inc(s_wd, 1)
            dve.wait_ge(s_wx, 1)
            ch(v.tensor_scalar(wden[:, :], wexp[:, :], 1.0, None, ALU.add))
            ch(v.reciprocal(wts[:, 0, :], wden[:, :]))
            v.tensor_tensor(wts[:, 1, :], wexp[:, :], wts[:, 0, :], ALU.mult).then_inc(s_wm, 1)

            expert_of = {}

            def expert_step(t, u, known):
                load_experts(dve, expert_of, (1, 3), t, u, known)
                if live(known, 0, ET):
                    dve.wait_ge(s_etp, t + 1)
                    if known is None or known >= 2:
                        dve.wait_ge(s_ehp, 2 * t - 2)
                    v.tensor_copy(exT[:, u % 2, :], etp16[u % 2]).then_inc(s_exT, 1)
                if live(known, 3, ET):
                    j, a, ex = t - 3, (u - 3) % R, expert_of[3]
                    dve.wait_ge(s_eyp, j + 1)
                    if known is None or known - 3 >= R:
                        dve.wait_ge(s_ysc[a], 32 * div(t, u, known, 3, R))
                    v.scalar_tensor_tensor(ysb[:, a, :, :], fold[(u - 3) % 2][:, :].rearrange("p (s n) -> p s n", s=2),
                                           sc2[:, bass.ds(ex, 1)], b2_bc[:, bass.ds(ex, 1), :].to_broadcast((P, 2, H)),
                                           ALU.mult, ALU.add).then_inc(s_ey, 1)
                if live(known, 1, ET):
                    j, r, ex = t - 1, (u - 1) % 2, expert_of[1]
                    dve.wait_ge(s_ehi, j + 1)
                    v.scalar_tensor_tensor(ehl[:, r, 1].rearrange("p t n -> p (t n)"), ehid[:, r].rearrange("p t n -> p (t n)"),
                                           shs[:, bass.ds(ex, 1)], ehl[:, r, 0].rearrange("p t n -> p (t n)"),
                                           ALU.mult, ALU.subtract).then_inc(s_elo, 1)
                    a = (u - 1) % R
                    if known is None or known - 1 >= R:
                        dve.wait_ge(s_ysc[a], 32 * div(t, u, known, 1, R))
                    v.scalar_tensor_tensor(enum[:, a, :], erow32[:, a, :, D + 1], texp[:, at(j)], erow32[:, a, :, D],
                                           ALU.not_equal, ALU.add).then_inc(s_idc, 1)

            dve.wait_ge(s_b2, 16)
            steps(dve, expert_step, 2, ET + 3, ET)

            def combine(k, kk, par):
                dve.wait_ge(s_yl[par], 16 * G * (kk + 1))
                for e in range(B):
                    t = B * k + e
                    v.scalar_tensor_tensor(flat(x_sb, t), yin[par][:, e, 0, :], wts[:, 0, at(t)], flat(x_sb, t), ALU.mult, ALU.add).then_inc(s_o1, 1)
                for e in range(B):
                    t = B * k + e
                    dve.wait_ge(s_o1, B * (k + 1))
                    v.scalar_tensor_tensor(flat(x_sb, t), yin[par][:, e, 1, :], wts[:, 1, at(t)], flat(x_sb, t), ALU.mult, ALU.add).then_inc(s_o2, 1)

            dve.wait_ge(s_wm, 1)
            with dve.Fori(0, NG // Y) as kk:
                for par in range(Y):
                    combine(Y * kk + par, kk, par)

        @block.tensor
        def _(pe):
            mm = nc.tensor.matmul
            PARTS = ((0, 0), (1, 0), (0, 1))

            pe.wait_ge(s_idt, 1)
            pe.wait_ge(s_w, 48)
            for w in range(2):
                for kt in range(KT):
                    for dt in range(KT):
                        last = nc.tensor.transpose(wps[w][:, kt * D + dt * P:kt * D + dt * P + P],
                                                   wraw[:, w, dt, kt * P:kt * P + P], identf[:, :])
                last.then_inc(s_wtp, 1)
            pe.wait_ge(s_wtc, 2)
            for dt in range(KT):
                for w in range(2):
                    for kt in range(KT):
                        last = mm(fold[dt][:, w * D:w * D + D], wT[:, w, kt, dt * P:dt * P + P], wraw[:, 2 + w, kt, :],
                                  start=(kt == 0), stop=(kt == KT - 1))
            last.then_inc(s_fold, 1)
            pe.wait_ge(s_bb, 2 * KT)
            for w in range(2):
                for kt in range(KT):
                    last = mm(cbank[:, 0:D], bbig[:, w, kt, :], wraw[:, 2 + w, kt, :],
                              start=(w + kt == 0), stop=(w + kt == KT))
            last.then_inc(s_cp, 1)

            def setup_step(t, u, known):
                if live(known, 1):
                    j, b_ = t - 1, tp16[(u - 1) % 2]
                    pe.wait_ge(s_lo, t)
                    if known is None or known >= 3:
                        pe.wait_ge(s_xT, t - 2)
                    for q in range(2 * KT):
                        last = nc.tensor.transpose(b_[:, q * P:q * P + P], hl[:, (u - 1) % 4, q * P:q * P + P], ident[:, :])
                    last.then_inc(s_tp, 1)
                if live(known, 3):
                    if known == 3:
                        pe.wait_ge(s_wf, 2)
                        pe.wait_ge(s_wsum, KT)
                    pe.wait_ge(s_xT, t - 2)
                    if known is None or known >= 7:
                        pe.wait_ge(s_zlo, t - 6)
                    n = 0
                    for xp, wp in PARTS:
                        for kt in range(KT):
                            last = mm(zbank[(u - 3) % 4][:, :], xT[:, (u - 3) % 4, (xp * KT + kt) * P:(xp * KT + kt + 1) * P],
                                      wf[:, wp, kt, :], start=(n == 0), stop=(n == 3 * KT - 1))
                            n += 1
                    last.then_inc(s_zp, 1)

            pe.wait_ge(s_idt, 2)
            steps(pe, setup_step, 2, NT + 3)

            def neighbours(u, half):
                n = NT // 2
                for i in range(n * half, n * half + n):
                    a = maskT8[u % 4][:, i // B, :, i % B]
                    mm(acc[u % 2][:, 0:D + 1], a, z_hi[:, i, :], start=(i == 0), stop=False)
                    last = mm(acc[u % 2][:, 0:D], a, z_lo[:, i, :], start=False, stop=(i == NT - 1))
                return last

            def main_step(t, u, known):
                if live(known, 0):
                    if known == 0:
                        pe.wait_ge(s_zlo, NT - 3)
                    pe.wait_ge(s_T, t + 1)
                    if known is None or known >= 2:
                        pe.wait_ge(s_ts, t - 1)
                    apart(pe)
                    neighbours(u, 0)
                if live(known, PT):
                    j = t - PT
                    pe.wait_ge(s_lo2, j + 1)
                    if known is None or known - PT >= 2:
                        pe.wait_ge(s_xT2, j - 1)
                    for q in range(2 * KT):
                        last = mm(tps[(u - PT) % 2][:, q * P:q * P + P],
                                  row16[:, at(j), q * P:q * P + P].rearrange("p o d -> p (o d)"), ident[:, :],
                                  start=True, stop=True)
                    last.then_inc(s_tp2, 1)
                if live(known, 0):
                    if known == 0:
                        pe.wait_ge(s_zlo, NT)
                    neighbours(u, 1).then_inc(s_mm, 1)
                if live(known, PL):
                    j = t - PL
                    pe.wait_ge(s_xT2, j + 1)
                    if known is None or known - PL >= 2:
                        pe.wait_ge(s_lg, j - 1)
                    n = 0
                    for xp, wp in PARTS:
                        for kt in range(KT):
                            last = mm(lbank[(u - PL) % 2][:, 0:E], xT[:, (u - PL) % 4, (xp * KT + kt) * P:(xp * KT + kt + 1) * P],
                                      wg_s[:, wp, kt, :], start=(n == 0), stop=(n == 3 * KT - 1))
                            n += 1
                    last.then_inc(s_lgp, 1)
                if u % B == PR % B and live(known, PR):
                    k = div(t, u, known, PR, B)
                    pe.wait_ge(s_both, k + 1)
                    mm(rbank[:, 0:B * E], upper[:, :], both[:, :, :].rearrange("p b e -> p (b e)"), start=True, stop=False)
                    mm(rbank[:, 0:B * E], ones[:, :], base[:, 0:B, :].rearrange("p b e -> p (b e)"), start=False, stop=True).then_inc(s_rkp, 1)

            pe.wait_ge(s_xT, NT)
            pe.wait_ge(s_cst, 4)
            pe.wait_ge(s_wf, 4)
            pe.wait_ge(s_cb, 1)
            steps(pe, main_step, 3, NT + PR - B + 1)
            mm(tbank[:, 0:E], ones[:, :], base[:, B, :], start=True, stop=True).then_inc(s_tot, 1)

            expert_of = {}

            def expert_step(t, u, known):
                load_experts(pe, expert_of, (1, 2), t, u, known)
                if live(known, 0, ET):
                    a = u % R
                    pe.wait_ge(s_er[a], 16 * (div(t, u, known, 0, R) + 1))
                    if known is None or known >= 2:
                        pe.wait_ge(s_exT, t - 1)
                    for q in range(2 * KT):
                        for s in range(2):
                            last = nc.tensor.transpose(etp16[u % 2][:, q * TT + s * P:q * TT + s * P + P],
                                                       erow[:, a, s, q * P:q * P + P], ident[:, :])
                    last.then_inc(s_etp, 1)
                if live(known, 1, ET):
                    j, r = t - 1, (u - 1) % 2
                    pe.wait_ge(s_exT, j + 1)
                    if known is None or known - 1 >= 2:
                        pe.wait_ge(s_eg, 2 * j - 2)
                    ex = expert_of[1]
                    for h in range(KT):
                        n = 0
                        for xp, wp in PARTS:
                            for kt in range(KT):
                                w = w12[:, bass.ds(ex, 1), 0, wp, kt, h * P:h * P + P].rearrange("p o n -> p (o n)")
                                last = mm(hps[2 * r + h][:, 0:TT], w, exT[:, r, (xp * KT + kt) * TT:(xp * KT + kt + 1) * TT],
                                          start=(n == 0), stop=(n == 3 * KT - 1))
                                n += 1
                        last.then_inc(s_ehp, 1)
                if live(known, 2, ET):
                    j, r = t - 2, (u - 2) % 2
                    ex = expert_of[2]
                    pe.wait_ge(s_elo, j + 1)
                    if known is None or known - 2 >= 2:
                        pe.wait_ge(s_ey, j - 1)
                    for s in range(2):
                        n = 0
                        for xp, wp in PARTS:
                            for kt in range(KT):
                                w = w12[:, bass.ds(ex, 1), 1, wp, kt, :].rearrange("p o n -> p (o n)")
                                last = mm(fold[r][:, s * H:s * H + H], ehl[:, r, xp, kt, s * P:s * P + P], w,
                                          start=(n == 0), stop=(n == 3 * KT - 1))
                                n += 1
                    last.then_inc(s_eyp, 1)

            pe.wait_ge(s_tab, 2)
            pe.wait_ge(s_el, 2 * E)
            steps(pe, expert_step, 1, ET + 2, ET)


_INS = ['x', 'adj', 'L0_gnn_W_self', 'L0_gnn_b_self', 'L0_gnn_W_nb', 'L0_gnn_b_nb', 'L0_gnn_W_comb', 'L0_gnn_b_comb',
        'L0_ffn_Wg', 'L0_ffn_bg', 'L0_ffn_W1', 'L0_ffn_b1', 'L0_ffn_W2', 'L0_ffn_b2']


def kernel(**inputs):
    import numpy as _np
    import concourse.bacc as _bacc
    from concourse import mybir as _mybir
    from concourse.bass_utils import run_bass_kernel_spmd as _run

    nc = _bacc.Bacc("TRN2", target_bir_lowering=False, num_devices=1)
    arrays, args = {}, []
    for name in _INS:
        a = _np.ascontiguousarray(inputs[name])
        arrays[f"in_{name}_dram"] = a
        args.append(nc.dram_tensor(f"in_{name}_dram", a.shape, _mybir.dt.from_np(a.dtype), kind="ExternalInput").ap())
    args.append(nc.dram_tensor("out_0_dram", inputs['x'].shape, _mybir.dt.float32, kind="ExternalOutput").ap())
    gnn_moe_kernel(nc, *args)
    r = _run(nc, [arrays], core_ids=[0])
    return r.results[0]["out_0_dram"]
```

```python
from contextlib import ExitStack

import concourse.bass as bass
from concourse import mybir

ALU = mybir.AluOpType
ACT = mybir.ActivationFunctionType
AX = mybir.AxisListType
F32 = mybir.dt.float32
F16 = mybir.dt.float16
F8 = mybir.dt.float8e4
I32 = mybir.dt.int32
U32 = mybir.dt.uint32
RED = bass.bass_isa.ReduceOp

P = 128
Q = 32
G = P // Q
EPS = 1e-5
XS = 2.0 ** 11


def gnn_moe_kernel(nc, x, adj, W_self, b_self, W_nb, b_nb, W_comb, b_comb, Wg, bg, W1, b1, W2, b2, out):
    N, D = x.shape
    E, _, H = W1.shape
    NT = N // P
    B = 4
    NG = NT // B
    KT = D // P
    NQ = N // G
    TT = 2 * P
    CAP = N // 2 + TT
    EH = (N + E * (TT - 1)) // TT
    ET = 2 * EH
    DUM = EH - N // TT
    PART = E * CAP + DUM * TT
    RW = 2 * D + 4
    assert D == H == 2 * P and N % (G * P) == 0 and E == 8 and B == 4

    xs_dram = nc.dram_tensor("dispatched", (2 * PART, RW), F16, kind="Internal").ap()
    yp_dram = nc.dram_tensor("pair_out", (2 * N, D), F32, kind="Internal").ap()

    x_v = x.rearrange("(g k c e) d -> g k c (e d)", g=G, k=NG, c=Q, e=B)
    out_v = out.rearrange("(g k c e) d -> g k c (e d)", g=G, k=NG, c=Q, e=B)
    adj_v = adj.rearrange("(b k r e) (g j) -> k e g r b j", b=G, k=NG, r=Q, e=B, g=G)
    yp_v = yp_dram[0:2 * N, :].rearrange("(g k c e) d -> g k c (e d)", g=G, k=NG, c=Q, e=2 * B)

    with ExitStack() as ctx:
        def sb(name, shape, dt):
            return ctx.enter_context(nc.sbuf_tensor(name, shape, dt))

        def sem(name):
            return ctx.enter_context(nc.semaphore(name))

        bank = [ctx.enter_context(nc.psum_tensor(f"bank{i}", [P, 512], F32)) for i in range(8)]
        acc = bank[0:2]
        hps = bank[0:2] + bank[6:8]
        zbank = bank[0:2] + bank[4:6]
        tps = bank[2:4]
        fold = bank[4:6]
        wps = bank[6:8]
        cbank = bank[7]
        lbank, rbank, tbank = bank[4:6], bank[7], bank[6]

        x_sb = sb("x_sb", [P, NT, D], F32)
        rows = sb("rows", [P, NT * RW], F16)
        row16 = rows[:, :].rearrange("p (t d) -> p t d", t=NT)
        self_sb = rows[:, :].bitcast(F32).rearrange("p (t d) -> p t d", t=NT)
        row32 = rows[:, :].bitcast(I32).rearrange("p (t d) -> p t d", t=NT)
        z_flat = sb("z_flat", [P, NT * (D + 1)], F16)
        z_hi = z_flat[:, :].rearrange("p (t d) -> p t d", t=NT)
        z_lo = sb("z_lo", [P, NT, D], F16)
        stage = sb("stage", [P, 4, 2, NQ], I32)
        mask = sb("mask", [P, 2, G, NQ], F8)
        maskT = sb("maskT", [P, 4, G * NQ], F8)
        w12 = sb("w12", [P, E, 2, 2, KT, H], F16)
        wst = sb("wst", [P, 2, KT, H], F32)
        b1c = sb("b1c", [P, E, KT], F32)
        wg_f = sb("wg_f", [P, KT, E], F32)
        wg_s = sb("wg_s", [P, 2, KT, E], F16)
        bg_bc = sb("bg_bc", [P, E], F32)
        const_bc = sb("const_bc", [P, D], F32)
        bcol = sb("bcol", [P, 2, KT], F32)
        diff = sb("diff", [P, P], I32)
        ident = sb("ident", [P, P], F16)
        identf = sb("identf", [P, P], F32)
        upper = sb("upper", [P, P], F16)
        ones = sb("ones", [P, P], F16)
        iota8 = sb("iota8", [P, E], F32)
        region = sb("region", [P, NG, E], F32)
        carry = sb("carry", [P, NG], F32)
        mhalf = sb("mhalf", [P, B], F32)
        st6 = sb("st6", [P, 2, B, 6], F32)
        ve = sb("ve", [P, 2, NT], F32)
        rs = sb("rs", [P, 2, NT], F32)
        nbx = sb("nbx", [P, NT], F32)
        mv2 = sb("mv2", [P, B, 2], F32)
        xh = sb("xh", [P, 2, D], F32)
        xT = sb("xT", [P, 4, 4 * P], F16)
        sdeg = sb("sdeg", [P, 4], F32)
        rdeg = sb("rdeg", [P, 4], F32)
        tsum = sb("tsum", [P, 2, D], F32)
        lg = sb("lg", [P, B, E], F32)
        top = sb("top", [P, B, 8], F32)
        tidx = sb("tidx", [P, B, 8], U32)
        tidf = sb("tidf", [P, B, 2], F32)
        hot = sb("hot", [P, 2, B, E], F32)
        both = sb("both", [P, B, E], F16)
        base = sb("base", [P, B + 1, E], F16)
        unused = sb("unused", [P, 1], F32)
        m100 = sb("m100", [P, 1], F32)
        rk = sb("rk", [P, B, E], F32)
        pick = sb("pick", [P, 2, B, E], F32)
        slotf = sb("slotf", [P, 2, B], F32)
        slot = sb("slot", [P, NT, 2], I32)
        m12 = sb("m12", [P, NT, 2], F32)
        wdif = sb("wdif", [P, NT], F32)
        wexp = sb("wexp", [P, NT], F32)
        wden = sb("wden", [P, NT], F32)
        wts = sb("wts", [P, 2, NT], F32)
        fmx = sb("fmx", [P, 3], F32)
        fmr = sb("fmr", [P, 3], F32)
        fcl = sb("fcl", [P, 2], F32)
        fp2 = sb("fp2", [P, 2], F32)
        fin = sb("fin", [P, 2], F32)
        scw = sb("scw", [P, 5], F32)
        emx = sb("emx", [P, 3], F32)
        emr = sb("emr", [P, 3], F32)
        ecl = sb("ecl", [P, 3], F32)
        ep2 = sb("ep2", [P, 3], F32)
        ein = sb("ein", [P, 3], F32)
        s12 = sb("s12", [P, 2], F32)
        sc1 = sb("sc1", [P, E], F32)
        shs = sb("shs", [P, E], F32)
        sc2 = sb("sc2", [P, E], F32)
        tio = sb("tio", [P, EH], F32)
        tior = sb("tior", [P, 2, EH], F32)
        q256 = sb("q256", [P, N // 2 // TT], F32)
        cntt = sb("cntt", [P, NG, E], F32)
        nti = sb("nti", [P, E], F32)
        cinc = sb("cinc", [P, E], F32)
        coef = sb("coef", [P, E], F32)
        onesE = sb("onesE", [P, E], F32)
        NQT = N // 2 // TT
        tge = sb("tge", [P, EH, E], F32)
        cmpq = tge[:, :, :].rearrange("p t e -> p (t e)")[:, 0:E * NQT].rearrange("p (e q) -> p e q", e=E)
        texp = sb("texp", [P, ET], F32)
        tjmp = sb("tjmp", [P, EH], F32)
        tab = sb("tab", [P, 2, ET], I32)
        padrow = sb("padrow", [P, 2, E], I32)
        enum = sb("enum", [P, 4, 2], I32)
        pad = sb("pad", [P, 2, RW], F16)
        pad32 = pad[:, :, :].rearrange("p s n -> p (s n)").bitcast(I32).rearrange("p (s n) -> p s n", s=2)

        setup_mem = w12[:, :, :, :, :, :].rearrange("p e w q t n -> p (e w q t n)").bitcast(F32)
        cuts = [0, 0]

        def cut_setup(n):
            cuts[0] += n
            assert cuts[0] <= 2 * E * KT * H
            return setup_mem[:, cuts[0] - n:cuts[0]]

        wraw = cut_setup(4 * KT * D).rearrange("p (w t n) -> p w t n", w=4, t=KT)
        wT = cut_setup(2 * KT * D).rearrange("p (w t n) -> p w t n", w=2, t=KT)
        bbig = cut_setup(2 * KT * P).rearrange("p (w t n) -> p w t n", w=2, t=KT)
        wf = cut_setup(2 * KT * D).bitcast(F16).rearrange("p (q t n) -> p q t n", q=2, t=KT)
        mv = cut_setup(2 * B).rearrange("p (t n) -> p t n", t=B)
        mean = cut_setup(NT)
        hl = cut_setup(4 * D).bitcast(F16).rearrange("p (a n) -> p a n", a=4)
        b2_bc = z_flat[:, :].bitcast(F32)[:, 0:E * H].rearrange("p (e n) -> p e n", e=E)

        ring = stage[:, :, :, :].rearrange("p a b c -> p (a b c)").bitcast(F32)

        def cut(n):
            cuts[1] += n
            assert cuts[1] <= 8 * NQ
            return ring[:, cuts[1] - n:cuts[1]]

        R = 4
        erow = cut(R * RW).bitcast(F16).rearrange("p (a s n) -> p a s n", a=R, s=2)
        erow32 = ring[:, 0:R * RW].bitcast(I32).rearrange("p (a s n) -> p a s n", a=R, s=2)
        ehid = cut(2 * TT * KT).rearrange("p (a t n) -> p a t n", a=2, t=KT)
        ehl = cut(2 * TT * KT).bitcast(F16).rearrange("p (a q t n) -> p a q t n", a=2, q=2, t=KT)
        exT = cut(2 * TT * KT).bitcast(F16).rearrange("p (a q n) -> p a (q n)", a=2, q=4)
        ysb = self_sb[:, 0:2 * R, 0:D].rearrange("p (a s) n -> p a s n", s=2)
        yin = [m.bitcast(F32).rearrange("p (a e k n) -> p a e k n", a=2, e=B, k=2)[:, a] for m in
               (z_lo[:, :, :].rearrange("p t n -> p (t n)"), maskT[:, :, :].rearrange("p a n -> p (a n)")) for a in range(2)]
        Y = len(yin)

        tp16 = [b_[:, 0:2 * P].bitcast(F16) for b_ in tps]
        etp16 = [b_[:, :].bitcast(F16) for b_ in tps]
        mask32 = [mask[:, i].rearrange("p b j -> p (b j)").bitcast(U32).rearrange("p (b k w) -> p b k w", b=G, k=NG) for i in range(2)]
        maskT32 = [maskT[:, i].bitcast(U32).rearrange("p (k b w) -> p b k w", b=G, k=NG) for i in range(4)]
        maskT8 = [maskT[:, i].rearrange("p (k m e) -> p k m e", k=NG, e=B) for i in range(4)]

        s_w, s_small, s_b12 = sem("weights_loaded"), sem("small_loaded"), sem("expert_biases_loaded")
        s_x = [sem("x0_loaded"), sem("x1_loaded"), sem("x2_loaded"), sem("x_rest_loaded")]
        s_iot, s_b2 = sem("table_iotas"), sem("b2_loaded")
        s_io, s_cst, s_idt, s_pad = sem("iotas"), sem("constants"), sem("identity"), sem("pad_rows")
        s_wtp, s_wtc, s_fold, s_wfh, s_scw = (sem(n) for n in (
            "weights_transposed", "wT_copied", "weights_folded", "fold_hi", "fold_scales"))
        s_fmx, s_fmr, s_fch, s_wf, s_bb, s_cp, s_cb = (sem(n) for n in (
            "fold_max", "fold_max_all", "fold_chain", "fold_split", "bias_spread", "const_product", "const_row"))
        s_st, s_ve, s_rs, s_nb = sem("stats_chain"), sem("variance"), sem("rstd"), sem("norm_scales")
        s_xh, s_hi, s_lo, s_tp, s_xT = sem("normalised"), sem("hi"), sem("lo"), sem("transposed"), sem("transposed_copied")
        s_zp, s_zhi, s_zlo = sem("setup_product"), sem("z_hi_made"), sem("z_lo_made")
        s_adj = [sem(f"adj_loaded{i}") for i in range(4)]
        s_mD, s_mA, s_T, s_mm = sem("mask_by_vector"), sem("mask_by_scalar"), sem("mask_transposed"), sem("neighbours_summed")
        s_dg, s_ts, s_x1, s_s2, s_ve2, s_rs2, s_rx2 = (sem(n) for n in (
            "degree_chain", "acc_read", "x1_made", "stats2_chain", "variance2", "rstd2", "scale2"))
        s_xh2, s_hi2, s_lo2, s_tp2, s_xT2, s_lgp = (sem(n) for n in (
            "normalised2", "hi2", "lo2", "transposed2", "transposed2_copied", "logits_product"))
        s_lg = sem("logits")
        s_rc, s_both, s_sl, s_rkp, s_slot = (sem(n) for n in ("route_chain", "one_hots", "slot_chain", "ranks", "slots"))
        s_sc = [sem("first_half_dispatched"), sem("second_half_dispatched")]
        s_ew, s_emx, s_emr, s_ech, s_es, s_eh, s_el = (sem(n) for n in (
            "expert_weights_loaded", "expert_max", "expert_max_all", "expert_chain", "expert_scales",
            "expert_hi", "expert_lo"))
        s_tch, s_tab, s_dum = (sem(n) for n in ("table_chain", "tables", "dummies_written"))
        s_padw = [sem("first_pads_written"), sem("second_pads_written")]
        s_wd, s_wx, s_wc, s_wm = sem("logit_gap"), sem("gap_exp"), sem("mix_chain"), sem("mix_weights")
        s_er = [sem(f"expert_rows_loaded{i}") for i in range(R)]
        s_etp, s_idc, s_exT, s_ehp, s_eg, s_ehi, s_elo, s_eyp, s_ey = (sem(n) for n in (
            "e_transposed", "e_numbers_copied", "e_transposed_copied", "e_hidden_product", "e_hidden", "e_hidden_hi", "e_hidden_lo",
            "e_out_product", "e_out"))
        s_ysc = [sem(f"outputs_scattered{i}") for i in range(R)]
        s_yl, s_o1, s_o2, s_out = [sem(f"pairs_loaded{i}") for i in range(Y)], sem("first_added"), sem("second_added"), sem("out_written")

        class Chain:

            def __init__(self, eng, s, base):
                self.eng, self.s, self.base, self.n = eng, s, base, 0

            def __call__(self, ins):
                self.n += 1
                ins.then_inc(self.s, 1)
                self.eng.wait_ge(self.s, self.base + self.n)

        def flat(a, t):
            return a[:, at(t), :].rearrange("p o n -> p (o n)")

        def spread(a, n=B):
            return a[:, :].rearrange("p (o e) -> p o e", o=1).to_broadcast((P, n, E))

        def at(t, n=1):
            return slice(t, t + n) if isinstance(t, int) else bass.ds(t, n)

        def div(t, u, known, lag, n):
            return (known - lag) // n if known is not None else (unroll[0] // n) * kreg[0] + (u - lag) // n

        kreg, unroll = [None], [B]

        X1, NORM, LOGIT, SCORE, HOT, SLOT = 3, 4, 5,7,10,12
        PT, PL, PR = 3,4,9
        EMAX, ESCALE, ESPLIT = 1, 2, 3
        GATE_STEPS = NT + SLOT - B + 1

        def steps(eng, step, peel, end, total=None, tail=0):
            total = NT if total is None else total
            run(eng, step, ((peel, total // B - tail),), end)

        def run(eng, step, loops, end, n=B):
            done = 0
            for a, b in loops:
                for t in range(done, n * a):
                    step(t, t, t)
                with eng.Fori(a, b) as k:
                    kreg[0], unroll[0] = k, n
                    for e in range(n):
                        step(n * k + e, e, None)
                done = n * b
            for t in range(done, end):
                step(t, t, t)

        TAB1 = 7

        def live(known, lag, total=None):
            total = NT if total is None else total
            return known is None or 0 <= known - lag < total

        def write_pad(eng, h, e):
            row = eng.value_load(padrow[0:1, h, e:e + 1], min_val=0, max_val=2 * PART - TT)
            eng.dma_start(xs_dram[bass.ds(row, TT), :].rearrange("(p s) n -> p (s n)", s=2),
                          pad[:, :, :].rearrange("p s n -> p (s n)")).then_inc(s_padw[h], 16)

        def load_experts(eng, held, lags, t, u, known):
            kept = {j: r for j, r in held.get("tiles", {}).items() if u > 0}
            held["tiles"] = {}
            for lag in lags:
                if live(known, lag, ET):
                    held[lag] = kept.get(u - lag)
                    if held[lag] is None:
                        held[lag] = eng.value_load(tab[0:1, 1, at(t - lag)], min_val=0, max_val=E - 1)
                    kept[u - lag] = held[lag]
            held["tiles"] = {j: r for j, r in kept.items() if j > u - max(lags)}

        def apart(eng):
            eng.nop(nofuse=True)

        block = ctx.enter_context(nc.Block())

        @block.sync
        def _(sp):
            def load_x(k, s):
                for g in range(G):
                    sp.dma_start(x_sb[Q * g:Q * g + Q, B * k:B * k + B, :].rearrange("p e d -> p (e d)"),
                                 x_v[g, k]).then_inc(s, 16)

            for k in range(NG):
                load_x(k, s_x[min(k, 3)])

            def load_adj(t, u, known):
                for h in range(2):
                    s = 2 * (u % 2) + h
                    if known is None or known >= 2:
                        sp.wait_ge((s_mD, s_mA)[h], t - 1)
                    for g in range(G):
                        if known is not None:
                            src = adj_v[t // B, t % B, g]
                        else:
                            src = adj_v[bass.ds(kreg[0], 1), u, g].rearrange("o r b j -> (o r) b j")
                        sp.dma_start(stage[Q * g:Q * g + Q, s], src[:, 2 * h:2 * h + 2, :]).then_inc(s_adj[s], 16)

            steps(sp, load_adj, 1, NT)

            sp.wait_ge(s_pad, 2)
            sp.wait_ge(s_tab, 2)
            for e in range(E):
                write_pad(sp, 0, e)
            sp.wait_ge(s_dum, 32 * DUM)
            sp.wait_ge(s_mA, NT)
            sp.wait_ge(s_mD, NT)

            def part_written(h):
                sp.wait_ge(s_padw[h], 16 * E)
                sp.wait_ge(s_sc[h], 16 * NT)

            def load_rows(t, u, known):
                if known == 0:
                    part_written(0)
                if known == EH:
                    part_written(1)
                a = u % R
                if known is None or known >= R:
                    sp.wait_ge(s_etp, t - R + 1)
                    sp.wait_ge(s_idc, t - R + 1)
                    apart(sp)
                row = sp.value_load(tab[0:1, 0, at(t)], min_val=0, max_val=2 * PART - TT)
                sp.dma_start(erow[:, a], xs_dram[bass.ds(row, TT), :].rearrange("(p s) n -> p s n", s=2)).then_inc(s_er[a], 16)
                if known == R - 1:
                    sp.wait_ge(s_mm, NT)
                    sp.dma_start(b2_bc[:, :, :].rearrange("p e n -> p (e n)"),
                                 b2.rearrange("(o e) n -> o (e n)", o=1).to_broadcast((P, E * H))).then_inc(s_b2, 16)
                if known in PADS:
                    if known == PADS[0]:
                        sp.wait_ge(s_tab, 4)
                    write_pad(sp, 1, PADS.index(known))
                if known in PAIRS:
                    load_pairs(PAIRS.index(known))

            PADS = range(6, 6 + E)
            PAIRS = range(EH + 7, EH + 7 + 2 * Y, 2)

            def load_pairs(k):
                first = k < NG // 2
                if k in (0, NG // 2):
                    for a in range(R):
                        sp.wait_ge(s_ysc[a], 32 * -(-((EH if first else ET) - a) // R))
                if not first:
                    sp.wait_ge(s_o2, B * (k - Y + 1))
                for g in range(G):
                    sp.dma_start(yin[k % Y][Q * g:Q * g + Q].rearrange("p e k n -> p (e k n)"), yp_v[g, k]).then_inc(s_yl[k % Y], 16)

            run(sp, load_rows, ((4, 5), (6, 7)), ET)
            for k in range(NG // 2, NG):
                load_pairs(k)
            sp.wait_ge(s_out, 16 * G * NG)

        @block.gpsimd
        def _(pool):
            gp = nc.gpsimd
            gp.iota(diff[:, :], [[1, P]], base=0, channel_multiplier=-1).then_inc(s_io, 1)
            gp.memset(mhalf[:, :], -0.5).then_inc(s_io, 1)
            small = dict(channel_multiplier=0, allow_small_or_imprecise_dtypes=True)
            gp.iota(iota8[:, :], [[1, E]], base=0, **small).then_inc(s_io, 1)
            gp.iota(region[:, :, :], [[PART, 2], [0, NG // 2], [CAP, E]], base=0, **small).then_inc(s_io, 1)
            gp.iota(q256[:, :], [[TT, N // 2 // TT]], base=0, **small).then_inc(s_iot, 1)
            gp.iota(tio[:, :], [[1, EH]], base=0, **small).then_inc(s_iot, 1)
            gp.iota(tior[:, :, :], [[PART, 2], [TT, EH]], base=0, **small).then_inc(s_iot, 1)
            for g in range(G):
                pool.wait_ge(s_io, 4 + g)
                gp.iota(row32[Q * g:Q * g + Q, :, D:D + 1], [[2 * P, NG], [2, B], [0, 1]], base=2 * NQ * g,
                        channel_multiplier=2 * B).then_inc(s_io, 1)
            pool.wait_ge(s_io, 8)
            gp.memset(pad[:, :, :], 0.0).then_inc(s_pad, 1)
            pool.wait_ge(s_pad, 1)
            gp.iota(pad32[:, :, D:D + 1], [[1, 2], [0, 1]], base=2 * N, channel_multiplier=2).then_inc(s_pad, 1)

            def rstd(k):
                pool.wait_ge(s_ve, k + 1)
                gp.tensor_tensor(rs[:, 0, at(B * k, B)], ve[:, 0, at(B * k, B)], mhalf[:, :], ALU.pow).then_inc(s_rs, 1)

            rstd(0)

            def expert_load(k):
                if k:
                    pool.wait_ge(s_el, 2 * k)
                for w, m in enumerate((W1, W2)):
                    pool.dma_start(wst[:, w], m[k].rearrange("(t p) n -> p t n", p=P)).then_inc(s_ew, 16)

            def expert_max(k):
                pool.wait_ge(s_emx, k + 1)
                gp.partition_all_reduce(emr[:, :], emx[:, :], P, RED.absmax).then_inc(s_emr, 1)

            def dispatch(t):
                pool.wait_ge(s_lo2, t + 1)
                pool.wait_ge(s_hi2, t + 1)
                pool.wait_ge(s_slot, t // B + 1)
                for c in range(2):
                    gp.indirect_dma_start(
                        out=xs_dram[:, :], out_offset=bass.IndirectOffsetOnAxis(ap=slot[:, t, c:c + 1], axis=0),
                        in_=self_sb[:, t, :].bitcast(F16), in_offset=None).then_inc(s_sc[t // (NT // 2)], 16)


            def setup_step(t, u, known):
                if known == 2:
                    rstd(1)
                    rstd(2)
                if known == 3:
                    pool.wait_ge(s_fmx, 3)
                    gp.partition_all_reduce(fmr[:, :], fmx[:, :], P, RED.absmax).then_inc(s_fmr, 1)
                pool.wait_ge(s_hi, t + 1)
                apart(pool)
                gp.tensor_tensor(hl[:, u % 4, D:2 * D], xh[:, u % 2, :], hl[:, u % 4, 0:D], ALU.subtract).then_inc(s_lo, 1)
                if u % B == 3 and (known is None or known < NT - 3 * B):
                    rstd(div(t, u, known, 0, B) + 3)

            steps(pool, setup_step, 1, NT, tail=3)
            pool.dma_start(b1c[:, :, :], b1.rearrange("e (t p) -> p e t", p=P), allow_slow_non_contiguous=True).then_inc(s_b12, 16)
            expert_load(0)
            pool.wait_ge(s_pad, 2)
            sent = 0
            for s in range(GATE_STEPS + 1):
                if 0 <= s - X1 < NT:
                    t = s - X1
                    pool.wait_ge(s_ve2, t + 1)
                    gp.tensor_tensor(rs[:, 1, t:t + 1], ve[:, 1, t:t + 1], mhalf[:, 0:1], ALU.pow).then_inc(s_rs2, 1)
                if 0 <= s - EMAX < NT and (s - EMAX) % B == 0:
                    expert_max((s - EMAX) // B)
                if 0 <= s - ESPLIT - 1 < NT - B and (s - ESPLIT - 1) % B == 0:
                    expert_load((s - ESPLIT - 1) // B + 1)
                if X1 <= s < X1 + 2 * DUM:
                    q = (s - X1) // DUM * PART + E * CAP + (s - X1) % DUM * TT
                    pool.dma_start(xs_dram[q:q + TT, :].rearrange("(p s) n -> p (s n)", s=2),
                                   pad[:, :, :].rearrange("p s n -> p (s n)")).then_inc(s_dum, 16)
                for _ in range(1 if s < NT - 2 else 2):
                    if sent < B * ((s - SLOT) // B + 1):
                        dispatch(sent)
                        sent += 1

            def scatter(t, u, known):
                a = u % R
                pool.wait_ge(s_idc, t + 1)
                pool.wait_ge(s_ey, t + 1)
                apart(pool)
                for s in range(2):
                    gp.indirect_dma_start(
                        out=yp_dram[:, :], out_offset=bass.IndirectOffsetOnAxis(ap=enum[:, a, s:s + 1], axis=0),
                        in_=ysb[:, a, s, :], in_offset=None, bounds_check=2 * N - 1, oob_is_err=False).then_inc(s_ysc[a], 16)

            steps(pool, scatter, 1, ET, ET)

        @block.scalar
        def _(act):
            sc = nc.scalar
            for w, m in enumerate((W_self, W_nb)):
                act.dma_start(wraw[:, w], m.rearrange("(t p) n -> p t n", p=P)).then_inc(s_w, 16)
            act.dma_start(wraw[:, 2:4].rearrange("p w t n -> p (w t) n"),
                          W_comb.rearrange("(t p) n -> p t n", p=P)).then_inc(s_w, 16)
            act.dma_start(bcol[:, 0, :], b_self.rearrange("(t p) -> p t", p=P), allow_slow_non_contiguous=True).then_inc(s_small, 16)
            act.dma_start(bcol[:, 1, :], b_nb.rearrange("(t p) -> p t", p=P), allow_slow_non_contiguous=True).then_inc(s_small, 16)
            act.dma_start(wg_f[:, :, :], Wg.rearrange("(t p) n -> p t n", p=P)).then_inc(s_small, 16)
            act.dma_start(const_bc[:, :], b_comb.rearrange("(o n) -> o n", o=1).to_broadcast((P, D))).then_inc(s_small, 16)
            act.dma_start(bg_bc[:, :], bg.rearrange("(o n) -> o n", o=1).to_broadcast((P, E))).then_inc(s_small, 16)

            for w in range(2):
                act.wait_ge(s_wtp, w + 1)
                sc.copy(wT[:, w].rearrange("p t n -> p (t n)"), wps[w][:, :]).then_inc(s_wtc, 1)

            def setup_step(t, u, known):
                if known == 3:
                    act.wait_ge(s_scw, 1)
                    for w in range(KT):
                        sc.activation(wf[:, 0, w, :], fold[w][:, :], ACT.Copy, scale=scw[:, 0:1]).then_inc(s_wfh, 1)
                if live(known, 0):
                    if known is None or known >= 2:
                        act.wait_ge(s_lo, t - 1)
                    act.wait_ge(s_nb, div(t, u, known, 0, B) + 1)
                    sc.activation(xh[:, u % 2, :], flat(x_sb, t), ACT.Identity, bias=nbx[:, at(t)],
                                  scale=rs[:, 0, at(t)]).then_inc(s_xh, 1)
                    if known is None or known >= 4:
                        act.wait_ge(s_tp, t - 3)
                    act.wait_ge(s_xh, t + 1)
                    sc.copy(hl[:, u % 4, 0:D], xh[:, u % 2, :]).then_inc(s_hi, 1)
                if live(known, 2):
                    act.wait_ge(s_tp, t - 1)
                    if known is None or known >= 6:
                        act.wait_ge(s_zp, t - 5)
                    sc.copy(xT[:, (u - 2) % 4, :], tp16[(u - 2) % 2]).then_inc(s_xT, 1)

                if known in AHEAD:
                    i = AHEAD.index(known)
                    masks(i, i, i)

            AHEAD = (NT - 2, NT)

            def masks(t, u, known):
                s = 2 * (u % 2) + 1
                act.wait_ge(s_adj[s], 64 * (div(t, u, known, 0, 2) + 1))
                if known is None or known >= 2:
                    act.wait_ge(s_T, t - 1)
                apart(act)
                sc.activation(mask[:, u % 2, 2:4, :], stage[:, s], ACT.Sigmoid, bias=m100[:, 0:1], scale=200.0,
                              saturate=False).then_inc(s_mA, 1)

            act.wait_ge(s_cst, 1)
            steps(act, setup_step, 2, NT + 4, tail=2)

            def main_step(t, u, known):
                if live(known, 0) and known not in (0, 1):
                    masks(t, u, known)
                if live(known, NORM):
                    act.wait_ge(s_xh2, t - NORM + 1)
                    sc.copy(row16[:, at(t - NORM), 0:D].rearrange("p o d -> p (o d)"), xh[:, (u - NORM) % 2, :]).then_inc(s_hi2, 1)
                if live(known, LOGIT):
                    act.wait_ge(s_tp2, t - LOGIT + 1)
                    if known is None or known - LOGIT >= 4:
                        act.wait_ge(s_lgp, t - LOGIT - 3)
                    sc.copy(xT[:, (u - LOGIT) % 4, :], tps[(u - LOGIT) % 2][:, :]).then_inc(s_xT2, 1)
                if u % B == ESPLIT % B and live(known, ESPLIT):
                    expert_hi(div(t, u, known, ESPLIT, B))

            def expert_hi(k):
                act.wait_ge(s_es, k + 1)
                for w in range(2):
                    sc.activation(w12[:, at(k), w, 0].rearrange("p o t n -> p (o t n)"), wst[:, w].rearrange("p t n -> p (t n)"),
                                  ACT.Copy, scale=s12[:, w:w + 1]).then_inc(s_eh, 1)

            act.wait_ge(s_zp, NT)
            steps(act, main_step, 3, NT + LOGIT)

            act.wait_ge(s_wd, 1)
            sc.activation(wexp[:, :], wdif[:, :], ACT.Exp).then_inc(s_wx, 1)
            sc.activation(unused[:, :], m100[:, :], ACT.Gelu)

            def expert_step(t, u, known):
                if known == TAB1:
                    act.wait_ge(s_tab, 4)
                ex = act.value_load(tab[0:1, 1, at(t)], min_val=0, max_val=E - 1)
                if known is None or known >= 2:
                    act.wait_ge(s_elo, t - 1)
                for h in range(KT):
                    act.wait_ge(s_ehp, 2 * t + h + 1)
                    sc.activation(ehid[:, u % 2, h, :], hps[2 * (u % 2) + h][:, 0:TT], ACT.Gelu,
                                  bias=b1c[:, bass.ds(ex, 1), h], scale=sc1[:, bass.ds(ex, 1)]).then_inc(s_eg, 1)
                act.wait_ge(s_eg, 2 * t + 2)
                if known is None or known >= 2:
                    act.wait_ge(s_eyp, t - 1)
                sc.activation(ehl[:, u % 2, 0].rearrange("p t n -> p (t n)"), ehid[:, u % 2].rearrange("p t n -> p (t n)"),
                              ACT.Copy, scale=shs[:, bass.ds(ex, 1)]).then_inc(s_ehi, 1)

            act.wait_ge(s_tab, 2)
            act.wait_ge(s_b12, 16)
            steps(act, expert_step, 2, ET, ET)

            with act.Fori(0, NG) as k:
                act.wait_ge(s_o2, B * k + B)
                for g in range(G):
                    act.dma_start(out_v[g, bass.ds(k, 1)].rearrange("o c n -> (o c) n"),
                                  x_sb[Q * g:Q * g + Q, bass.ds(B * k, B), :].rearrange("p e d -> p (e d)")).then_inc(s_out, 16)

        @block.vector
        def _(dve):
            v = nc.vector

            def stats_a(k):
                for e in range(B):
                    v.bn_stats(st6[:, 0, e, :], flat(x_sb, B * k + e)).then_inc(s_st, 1)
                dve.wait_ge(s_st, 2 * B * k + B)
                for e in range(B):
                    if e == 0:
                        apart(dve)
                    v.bn_aggr(mv[:, e, :], st6[:, 0, e, :]).then_inc(s_st, 1)
                dve.wait_ge(s_st, 2 * B * (k + 1))
                v.tensor_copy(mean[:, at(B * k, B)], mv[:, :, 0])
                v.tensor_scalar(ve[:, 0, at(B * k, B)], mv[:, :, 1],
                                EPS, XS ** -2, ALU.add, ALU.mult).then_inc(s_ve, 1)

            def stats_b(k):
                dve.wait_ge(s_rs, k + 1)
                v.scalar_tensor_tensor(nbx[:, at(B * k, B)], mean[:, at(B * k, B)],
                                       -1.0, rs[:, 0, at(B * k, B)], ALU.mult, ALU.mult).then_inc(s_nb, 1)

            def powers(ch, out_, inv, mx):
                ch(v.tensor_scalar(mx, mx, 1e-30, None, ALU.max))
                ch(v.tensor_scalar(out_.bitcast(U32), mx.bitcast(U32), 0x7F800000, None, ALU.bitwise_and))
                ch(v.reciprocal(inv, out_))

            dve.wait_ge(s_io, 8)
            v.tensor_scalar(identf[:, :], diff[:, :], 0.0, None, ALU.is_equal).then_inc(s_idt, 1)
            v.tensor_scalar(ident[:, :], diff[:, :], 0.0, None, ALU.is_equal).then_inc(s_idt, 1)
            v.tensor_scalar(upper[:, :], diff[:, :], 0.0, None, ALU.is_gt).then_inc(s_idt, 1)
            v.memset(ones[:, :], 1.0).then_inc(s_idt, 1)
            v.memset(m100[:, :], -100.0).then_inc(s_cst, 1)
            v.memset(onesE[:, :], 1.0).then_inc(s_cst, 1)
            v.memset(z_hi[:, :, D:D + 1], 1.0).then_inc(s_cst, 1)
            v.memset(base[:, :, :], 0.0)
            v.memset(carry[:, :], 1.0).then_inc(s_cst, 1)
            dve.wait_ge(s_cst, 4)
            for k in (0, NG // 2):
                v.memset(carry[:, k:k + 1], 0.0).then_inc(s_cst, 1)
            dve.wait_ge(s_x[0], 16 * G)
            stats_a(0)

            dve.wait_ge(s_small, 16 * 5)
            dve.wait_ge(s_idt, 4)
            for w in range(2):
                for t in range(KT):
                    v.tensor_scalar(bbig[:, w, t, :], ones[:, :], bcol[:, w, t:t + 1], None, ALU.mult).then_inc(s_bb, 1)
            stats_b(0)
            v.tensor_reduce(fmx[:, 1:2], wg_f[:, :, :].rearrange("p t n -> p (t n)"), AX.X, ALU.max, apply_absolute_value=True).then_inc(s_fmx, 1)
            for k in (1, 2):
                dve.wait_ge(s_x[k], 16 * G)
                stats_a(k)
            for t in range(KT):
                dve.wait_ge(s_fold, t + 1)
                v.tensor_reduce(fmx[:, 2 * t:2 * t + 1], fold[t][:, :], AX.X, ALU.max, apply_absolute_value=True).then_inc(s_fmx, 1)
            dve.wait_ge(s_cp, 1)
            v.tensor_tensor(const_bc[:, :], cbank[:, 0:D], const_bc[:, :], ALU.add).then_inc(s_cb, 1)
            stats_b(1)
            stats_b(2)
            dve.wait_ge(s_fmr, 1)
            ch = Chain(dve, s_fch, 0)
            ch(v.tensor_tensor(fmr[:, 0:1], fmr[:, 0:1], fmr[:, 2:3], ALU.max))
            powers(ch, fp2[:, :], fin[:, :], fmr[:, 0:2])
            v.tensor_scalar(scw[:, 0:2], fin[:, :], 2.0 ** 14, None, ALU.mult).then_inc(s_scw, 1)
            v.tensor_scalar(scw[:, 2:4], fp2[:, :], 2.0 ** -14 / XS, None, ALU.mult)
            v.tensor_scalar(scw[:, 4:5], fin[:, 0:1], 2.0 ** 6, None, ALU.mult).then_inc(s_scw, 1)
            dve.wait_ge(s_scw, 2)
            for t in range(KT):
                dve.wait_ge(s_wfh, t + 1)
                v.scalar_tensor_tensor(wf[:, 1, t, :], fold[t][:, :], scw[:, 0:1], wf[:, 0, t, :], ALU.mult, ALU.subtract).then_inc(s_wf, 1)
            v.tensor_scalar(wg_s[:, 0], wg_f[:, :, :], scw[:, 1:2], None, ALU.mult).then_inc(s_wf, 1)
            dve.wait_ge(s_wf, KT + 1)
            v.scalar_tensor_tensor(wg_s[:, 1], wg_f[:, :, :], scw[:, 1:2], wg_s[:, 0], ALU.mult, ALU.subtract).then_inc(s_wf, 1)

            def setup_step(t, u, known):
                nxt = div(t, u, known, 0, B) + 3
                if u % B == 0 and (known is None or B <= known < NT - 2 * B):
                    stats_b(nxt - 1)
                if u % B == 0 and (known is None or known < NT - 3 * B):
                    if known == 0:
                        dve.wait_ge(s_x[3], 16 * G * (NG - 3))
                    stats_a(nxt)
                if live(known, 5):
                    b_ = zbank[(u - 5) % 4]
                    dve.wait_ge(s_zp, t - 4)
                    v.tensor_scalar(z_hi[:, at(t - 5), 0:D].rearrange("p o d -> p (o d)"), b_[:, D:2 * D],
                                    2.0 ** -19, None, ALU.mult).then_inc(s_zhi, 1)
                    v.scalar_tensor_tensor(self_sb[:, at(t - 5), 0:D].rearrange("p o d -> p (o d)"), b_[:, 0:D],
                                           scw[:, 2:3], const_bc[:, :], ALU.mult, ALU.add)
                    dve.wait_ge(s_zhi, t - 4)
                    v.scalar_tensor_tensor(flat(z_lo, t - 5), b_[:, D:2 * D], 2.0 ** -19,
                                           z_hi[:, at(t - 5), 0:D].rearrange("p o d -> p (o d)"),
                                           ALU.mult, ALU.subtract).then_inc(s_zlo, 1)
                if known in AHEAD:
                    i = AHEAD.index(known)
                    masks(i, i, i)
                if known in AHEAD_T:
                    i = AHEAD_T.index(known)
                    mask_transpose(i, i, i)

            AHEAD, AHEAD_T = (NT - 2, NT), (NT + 1, NT + 3)

            def masks(t, u, known):
                s = 2 * (u % 2)
                if known is None or known >= 2:
                    dve.wait_ge(s_T, t - 1)
                dve.wait_ge(s_adj[s], 64 * (div(t, u, known, 0, 2) + 1))
                apart(dve)
                v.tensor_scalar(mask[:, u % 2, 0:2, :], stage[:, s], 0.0, None, ALU.is_gt, saturate=False).then_inc(s_mD, 1)

            def mask_transpose(t, u, known):
                dve.wait_ge(s_mD, t + 1)
                dve.wait_ge(s_mA, t + 1)
                if known is None or known >= 4:
                    dve.wait_ge(s_mm, t - 3)
                v.transpose(maskT32[u % 4], mask32[u % 2]).then_inc(s_T, 1)

            dve.wait_ge(s_cb, 1)
            steps(dve, setup_step, 2, NT + 5, tail=3)

            def main_step(t, u, known):
                if live(known, NORM):
                    j = t - NORM
                    dve.wait_ge(s_rs2, j + 1)
                    if known is None or known - NORM >= 2:
                        dve.wait_ge(s_hi2, j - 1)
                    v.tensor_scalar(xh[:, (u - NORM) % 2, :], flat(x_sb, j), mv2[:, (u - NORM) % 4, 0:1], rs[:, 1, at(j)],
                                    ALU.subtract, ALU.mult).then_inc(s_xh2, 1)
                if live(known, X1):
                    j, p, r = t - X1, acc[(u - X1) % 2], (u - X1) % 4
                    dve.wait_ge(s_mm, j + 1)
                    v.tensor_scalar(sdeg[:, r:r + 1], p[:, D:D + 1], 1.0, scw[:, 4:5], ALU.max, ALU.mult).then_inc(s_dg, 1)
                if live(known, 0) and known not in (0, 1):
                    masks(t, u, known)
                if live(known, X1):
                    dve.wait_ge(s_dg, 2 * j + 1)
                    v.reciprocal(rdeg[:, r:r + 1], sdeg[:, r:r + 1]).then_inc(s_dg, 1)
                    dve.wait_ge(s_dg, 2 * j + 2)
                    v.scalar_tensor_tensor(tsum[:, r % 2, :], p[:, 0:D], rdeg[:, r:r + 1],
                                           self_sb[:, at(j), 0:D].rearrange("p o d -> p (o d)"), ALU.mult, ALU.add).then_inc(s_ts, 1)
                if live(known, NORM):
                    i = t - NORM
                    dve.wait_ge(s_hi2, i + 1)
                    v.tensor_tensor(row16[:, at(i), D:2 * D].rearrange("p o d -> p (o d)"), xh[:, (u - NORM) % 2, :],
                                    row16[:, at(i), 0:D].rearrange("p o d -> p (o d)"), ALU.subtract).then_inc(s_lo2, 1)
                if live(known, X1):
                    dve.wait_ge(s_ts, j + 1)
                    v.scalar_tensor_tensor(flat(x_sb, j), tsum[:, r % 2, :], 0.0, flat(x_sb, j), ALU.max, ALU.add).then_inc(s_x1, 1)
                if live(known, 0) and known not in (0, 1):
                    mask_transpose(t, u, known)
                if live(known, X1):
                    dve.wait_ge(s_x1, j + 1)
                    apart(dve)
                    v.bn_stats(st6[:, 1, r, :], flat(x_sb, j)).then_inc(s_s2, 1)
                    dve.wait_ge(s_s2, 2 * j + 1)
                    apart(dve)
                    v.bn_aggr(mv2[:, r, :], st6[:, 1, r, :]).then_inc(s_s2, 1)
                    dve.wait_ge(s_s2, 2 * j + 2)
                    v.tensor_scalar(ve[:, 1, at(j)], mv2[:, r, 1:2], EPS, XS ** -2, ALU.add, ALU.mult).then_inc(s_ve2, 1)
                if u % B == EMAX % B and live(known, EMAX):
                    expert_max(div(t, u, known, EMAX, B))
                if u % B == ESCALE % B and live(known, ESCALE):
                    expert_scales(div(t, u, known, ESCALE, B))
                if u % B == ESPLIT % B and live(known, ESPLIT):
                    expert_lo(div(t, u, known, ESPLIT, B))
                if live(known, SCORE):
                    i = t - SCORE
                    dve.wait_ge(s_lgp, i + 1)
                    v.scalar_tensor_tensor(lg[:, (u - SCORE) % B, :], lbank[(u - SCORE) % 2][:, 0:E], scw[:, 3:4], bg_bc[:, :],
                                           ALU.mult, ALU.add).then_inc(s_lg, 1)
                if u % B == HOT % B and live(known, HOT):
                    choose(div(t, u, known, HOT, B))
                if u % B == SLOT % B and live(known, SLOT):
                    slots(div(t, u, known, SLOT, B))
                if known == NT - 3:
                    table(0)

            def expert_max(k):
                dve.wait_ge(s_ew, 32 * (k + 1))
                dve.wait_ge(s_b12, 16)
                for w in range(2):
                    v.tensor_reduce(emx[:, w:w + 1], wst[:, w].rearrange("p t n -> p (t n)"), AX.X, ALU.max, apply_absolute_value=True)
                v.tensor_reduce(emx[:, 2:3], flat(b1c, k), AX.X, ALU.max, apply_absolute_value=True).then_inc(s_emx, 1)

            def expert_scales(k):
                dve.wait_ge(s_emr, k + 1)
                ch = Chain(dve, s_ech, 4 * k)
                v.tensor_copy(ecl[:, 0:2], emr[:, 0:2])
                ch(v.scalar_tensor_tensor(ecl[:, 2:3], emr[:, 0:1], float(D), emr[:, 2:3], ALU.mult, ALU.add))
                powers(ch, ep2[:, :], ein[:, :], ecl[:, :])
                v.tensor_scalar(sc1[:, at(k)], ep2[:, 0:1], 2.0 ** -14 / XS, None, ALU.mult)
                v.tensor_scalar(shs[:, at(k)], ein[:, 2:3], 2.0 ** 14, None, ALU.mult)
                v.scalar_tensor_tensor(sc2[:, at(k)], ep2[:, 2:3], 2.0 ** -28, ep2[:, 1:2], ALU.mult, ALU.mult)
                v.tensor_scalar(s12[:, :], ein[:, 0:2], 2.0 ** 14, None, ALU.mult).then_inc(s_es, 1)

            def expert_lo(k):
                dve.wait_ge(s_eh, 2 * k + 2)
                for w in range(2):
                    v.scalar_tensor_tensor(w12[:, at(k), w, 1].rearrange("p o t n -> p (o t n)"),
                                           wst[:, w].rearrange("p t n -> p (t n)"), s12[:, w:w + 1],
                                           w12[:, at(k), w, 0].rearrange("p o t n -> p (o t n)"),
                                           ALU.mult, ALU.subtract).then_inc(s_el, 1)

            def choose(k):
                dve.wait_ge(s_lg, B * (k + 1))
                if not isinstance(k, int) or k:
                    dve.wait_ge(s_both, k)
                ch = Chain(dve, s_rc, HN * k)
                apart(dve)
                for b_ in range(B):
                    last = v.max(top[:, b_, :], lg[:, b_, :])
                ch(last)
                v.tensor_copy(m12[:, at(B * k, B), :], top[:, :, 0:2])
                for b_ in range(B):
                    last = v.max_index(tidx[:, b_, :], top[:, b_, :], lg[:, b_, :])
                ch(last)
                ch(v.tensor_copy(tidf[:, :, :], tidx[:, :, 0:2]))
                v.tensor_copy(row32[:, at(B * k, B), D + 1:D + 2], tidf[:, :, 0:1])
                for c in range(2):
                    last = v.tensor_tensor(hot[:, c], spread(iota8), tidf[:, :, c:c + 1].to_broadcast((P, B, E)), ALU.is_equal)
                ch(last)
                ch(v.tensor_tensor(both[:, :, :], hot[:, 0], hot[:, 1], ALU.add))
                ch(v.tensor_scalar(base[:, 0, :], base[:, B, :], carry[:, at(k)], None, ALU.mult))
                for b_ in range(B - 1):
                    ch(v.tensor_tensor(base[:, b_ + 1, :], base[:, b_, :], both[:, b_, :], ALU.add))
                v.tensor_tensor(base[:, B, :], base[:, B - 1, :], both[:, B - 1, :], ALU.add).then_inc(s_both, 1)
                assert ch.n == HN

            HN = 6 + B - 1

            def slots(k):
                dve.wait_ge(s_rkp, k + 1)
                ch = Chain(dve, s_sl, 3 * k)
                ch(v.tensor_tensor(rk[:, :, :], rbank[:, 0:B * E].rearrange("p (b e) -> p b e", b=B),
                                   region[:, at(k), :].to_broadcast((P, B, E)), ALU.add))
                v.tensor_copy(cntt[:, at(k), :].rearrange("p o e -> p (o e)"), tbank[:, 0:E])
                for c in range(2):
                    last = v.tensor_tensor(pick[:, c], hot[:, c], rk[:, :, :], ALU.mult)
                ch(last)
                ch(v.tensor_reduce(slotf[:, :, :], pick[:, :, :, :], AX.X, ALU.add))
                v.tensor_copy(slot[:, at(B * k, B), :].rearrange("p t c -> p c t"), slotf[:, :, :]).then_inc(s_slot, 1)

            def table(h):
                dve.wait_ge(s_iot, 3)
                ch = Chain(dve, s_tch, 9 * h)
                count, mine = cntt[:, NG // 2 * (h + 1) - 1, :], slice(EH * h, EH * h + EH)
                ch(v.tensor_tensor(cmpq[:, :, :], count.rearrange("p (e o) -> p e o", o=1).to_broadcast((P, E, NQT)),
                                   q256[:, :].rearrange("p (o q) -> p o q", o=1).to_broadcast((P, E, NQT)), ALU.is_gt))
                ch(v.tensor_reduce(nti[:, :], cmpq[:, :, :], AX.X, ALU.add))
                ch(v.tensor_tensor_scan(cinc[:, :], onesE[:, :], nti[:, :], 0.0, ALU.mult, ALU.add))
                ch(v.tensor_scalar(coef[:, :], nti[:, :], -float(TT), float(CAP), ALU.mult, ALU.add))
                ch(v.tensor_tensor(tge[:, :, :], tio[:, :].rearrange("p (t o) -> p t o", o=1).to_broadcast((P, EH, E)),
                                   spread(cinc, EH), ALU.is_ge))
                ch(v.tensor_reduce(texp[:, mine], tge[:, :, :], AX.X, ALU.add))
                ch(v.tensor_tensor(tge[:, :, :], tge[:, :, :], spread(coef, EH), ALU.mult))
                ch(v.tensor_reduce(tjmp[:, :], tge[:, :, :], AX.X, ALU.add))
                v.tensor_tensor(tab[:, 0, mine], tior[:, h, :], tjmp[:, :], ALU.add)
                ch(v.tensor_scalar(tab[:, 1, mine], texp[:, mine], float(E - 1), None, ALU.min))
                v.tensor_tensor(padrow[:, h, :], count, region[:, NG // 2 * h, :], ALU.add).then_inc(s_tab, 2)

            steps(dve, main_step, 4, GATE_STEPS + 1, tail=1)

            v.tensor_tensor(wdif[:, :], m12[:, :, 1], m12[:, :, 0], ALU.subtract).then_inc(s_wd, 1)

            def mix_weights():
                dve.wait_ge(s_wx, 1)
                ch = Chain(dve, s_wc, 0)
                ch(v.tensor_scalar(wden[:, :], wexp[:, :], 1.0, None, ALU.add))
                ch(v.reciprocal(wts[:, 0, :], wden[:, :]))
                v.tensor_tensor(wts[:, 1, :], wexp[:, :], wts[:, 0, :], ALU.mult).then_inc(s_wm, 1)

            expert_of = {}

            def expert_step(t, u, known):
                if known == TAB1:
                    dve.wait_ge(s_tab, 4)
                load_experts(dve, expert_of, (1, 3), t, u, known)
                if live(known, 0, ET):
                    dve.wait_ge(s_etp, t + 1)
                    if known is None or known >= 2:
                        dve.wait_ge(s_ehp, 2 * t - 2)
                    v.tensor_copy(exT[:, u % 2, :], etp16[u % 2]).then_inc(s_exT, 1)
                if live(known, 3, ET):
                    j, a, ex = t - 3, (u - 3) % R, expert_of[3]
                    if known == 3:
                        dve.wait_ge(s_b2, 16)
                    dve.wait_ge(s_eyp, j + 1)
                    if known is None or known - 3 >= R:
                        dve.wait_ge(s_ysc[a], 32 * div(t, u, known, 3, R))
                    v.scalar_tensor_tensor(ysb[:, a, :, :], fold[(u - 3) % 2][:, :].rearrange("p (s n) -> p s n", s=2),
                                           sc2[:, bass.ds(ex, 1)], b2_bc[:, bass.ds(ex, 1), :].to_broadcast((P, 2, H)),
                                           ALU.mult, ALU.add).then_inc(s_ey, 1)
                if live(known, 1, ET):
                    j, r, ex = t - 1, (u - 1) % 2, expert_of[1]
                    dve.wait_ge(s_ehi, j + 1)
                    v.scalar_tensor_tensor(ehl[:, r, 1].rearrange("p t n -> p (t n)"), ehid[:, r].rearrange("p t n -> p (t n)"),
                                           shs[:, bass.ds(ex, 1)], ehl[:, r, 0].rearrange("p t n -> p (t n)"),
                                           ALU.mult, ALU.subtract).then_inc(s_elo, 1)
                    a = (u - 1) % R
                    if known is None or known - 1 >= R:
                        dve.wait_ge(s_ysc[a], 32 * div(t, u, known, 1, R))
                    v.scalar_tensor_tensor(enum[:, a, :], erow32[:, a, :, D + 1], texp[:, at(j)], erow32[:, a, :, D],
                                           ALU.not_equal, ALU.add).then_inc(s_idc, 1)
                if known == 2:
                    mix_weights()
                if known == 3:
                    table(1)
                if known in range(COMBINE, COMBINE + NT // 2):
                    combine(known - COMBINE)

            COMBINE = EH + 8

            def combine(t, n=1):
                k = t // B
                dve.wait_ge(s_yl[k % Y], 16 * G * (k // Y + 1))
                for c, done in ((0, s_o1), (1, s_o2)):
                    for i in range(t, t + n):
                        if c:
                            dve.wait_ge(s_o1, i + 1)
                        v.scalar_tensor_tensor(flat(x_sb, i), yin[k % Y][:, i % B, c, :], wts[:, c, at(i)], flat(x_sb, i),
                                               ALU.mult, ALU.add).then_inc(done, 1)

            run(dve, expert_step, ((2, COMBINE // B),), ET + 3)
            for t in range(NT // 2, NT, 2):
                combine(t, 2)

        @block.tensor
        def _(pe):
            mm = nc.tensor.matmul
            PARTS = ((0, 0), (1, 0), (0, 1))

            pe.wait_ge(s_idt, 1)
            pe.wait_ge(s_w, 48)
            for w in range(2):
                for kt in range(KT):
                    for dt in range(KT):
                        last = nc.tensor.transpose(wps[w][:, kt * D + dt * P:kt * D + dt * P + P],
                                                   wraw[:, w, dt, kt * P:kt * P + P], identf[:, :])
                last.then_inc(s_wtp, 1)
            pe.wait_ge(s_wtc, 2)
            for dt in range(KT):
                for w in range(2):
                    for kt in range(KT):
                        last = mm(fold[dt][:, w * D:w * D + D], wT[:, w, kt, dt * P:dt * P + P], wraw[:, 2 + w, kt, :],
                                  start=(kt == 0), stop=(kt == KT - 1))
                last.then_inc(s_fold, 1)
            pe.wait_ge(s_bb, 2 * KT)
            for w in range(2):
                for kt in range(KT):
                    last = mm(cbank[:, 0:D], bbig[:, w, kt, :], wraw[:, 2 + w, kt, :],
                              start=(w + kt == 0), stop=(w + kt == KT))
            last.then_inc(s_cp, 1)

            def setup_step(t, u, known):
                if live(known, 1):
                    j, b_ = t - 1, tp16[(u - 1) % 2]
                    pe.wait_ge(s_lo, t)
                    if known is None or known >= 3:
                        pe.wait_ge(s_xT, t - 2)
                    for q in range(2 * KT):
                        last = nc.tensor.transpose(b_[:, q * P:q * P + P], hl[:, (u - 1) % 4, q * P:q * P + P], ident[:, :])
                    last.then_inc(s_tp, 1)
                if live(known, 3):
                    if known == 3:
                        pe.wait_ge(s_wf, KT)
                    pe.wait_ge(s_xT, t - 2)
                    if known is None or known >= 7:
                        pe.wait_ge(s_zlo, t - 6)
                    n = 0
                    for xp, wp in PARTS:
                        for kt in range(KT):
                            last = mm(zbank[(u - 3) % 4][:, :], xT[:, (u - 3) % 4, (xp * KT + kt) * P:(xp * KT + kt + 1) * P],
                                      wf[:, wp, kt, :], start=(n == 0), stop=(n == 3 * KT - 1))
                            n += 1
                    last.then_inc(s_zp, 1)

            pe.wait_ge(s_idt, 2)
            steps(pe, setup_step, 2, NT + 3)

            def neighbours(u, half):
                n = NT // 2
                for i in range(n * half, n * half + n):
                    a = maskT8[u % 4][:, i // B, :, i % B]
                    mm(acc[u % 2][:, 0:D + 1], a, z_hi[:, i, :], start=(i == 0), stop=False)
                    last = mm(acc[u % 2][:, 0:D], a, z_lo[:, i, :], start=False, stop=(i == NT - 1))
                return last

            def main_step(t, u, known):
                if live(known, 0):
                    if known == 0:
                        pe.wait_ge(s_zlo, NT - 3)
                    pe.wait_ge(s_T, t + 1)
                    if known is None or known >= 2:
                        pe.wait_ge(s_ts, t - 1)
                    apart(pe)
                    neighbours(u, 0)
                if live(known, PT):
                    j = t - PT
                    pe.wait_ge(s_lo2, j + 1)
                    if known is None or known - PT >= 2:
                        pe.wait_ge(s_xT2, j - 1)
                    for q in range(2 * KT):
                        last = mm(tps[(u - PT) % 2][:, q * P:q * P + P],
                                  row16[:, at(j), q * P:q * P + P].rearrange("p o d -> p (o d)"), ident[:, :],
                                  start=True, stop=True)
                    last.then_inc(s_tp2, 1)
                if live(known, 0):
                    if known == 0:
                        pe.wait_ge(s_zlo, NT)
                    neighbours(u, 1).then_inc(s_mm, 1)
                if live(known, PL):
                    j = t - PL
                    pe.wait_ge(s_xT2, j + 1)
                    if known is None or known - PL >= 2:
                        pe.wait_ge(s_lg, j - 1)
                    n = 0
                    for xp, wp in PARTS:
                        for kt in range(KT):
                            last = mm(lbank[(u - PL) % 2][:, 0:E], xT[:, (u - PL) % 4, (xp * KT + kt) * P:(xp * KT + kt + 1) * P],
                                      wg_s[:, wp, kt, :], start=(n == 0), stop=(n == 3 * KT - 1))
                            n += 1
                    last.then_inc(s_lgp, 1)
                if u % B == PR % B and live(known, PR):
                    k = div(t, u, known, PR, B)
                    pe.wait_ge(s_both, k + 1)
                    mm(rbank[:, 0:B * E], upper[:, :], both[:, :, :].rearrange("p b e -> p (b e)"), start=True, stop=False)
                    mm(rbank[:, 0:B * E], ones[:, :], base[:, 0:B, :].rearrange("p b e -> p (b e)"), start=False, stop=True)
                    mm(tbank[:, 0:E], ones[:, :], base[:, B, :], start=True, stop=True).then_inc(s_rkp, 1)

            pe.wait_ge(s_xT, NT)
            pe.wait_ge(s_cst, 6)
            pe.wait_ge(s_wf, KT + 2)
            pe.wait_ge(s_cb, 1)
            steps(pe, main_step, 3, NT + PR - B + 1)

            expert_of = {}

            def expert_step(t, u, known):
                if known == TAB1:
                    pe.wait_ge(s_tab, 4)
                load_experts(pe, expert_of, (1, 2), t, u, known)
                if live(known, 0, ET):
                    a = u % R
                    pe.wait_ge(s_er[a], 16 * (div(t, u, known, 0, R) + 1))
                    for q in range(2 * KT):
                        for s in range(2):
                            last = nc.tensor.transpose(etp16[u % 2][:, q * TT + s * P:q * TT + s * P + P],
                                                       erow[:, a, s, q * P:q * P + P], ident[:, :])
                    last.then_inc(s_etp, 1)
                if live(known, 1, ET):
                    j, r = t - 1, (u - 1) % 2
                    pe.wait_ge(s_exT, j + 1)
                    ex = expert_of[1]
                    for h in range(KT):
                        n = 0
                        for xp, wp in PARTS:
                            for kt in range(KT):
                                w = w12[:, bass.ds(ex, 1), 0, wp, kt, h * P:h * P + P].rearrange("p o n -> p (o n)")
                                last = mm(hps[2 * r + h][:, 0:TT], w, exT[:, r, (xp * KT + kt) * TT:(xp * KT + kt + 1) * TT],
                                          start=(n == 0), stop=(n == 3 * KT - 1))
                                n += 1
                        last.then_inc(s_ehp, 1)
                if live(known, 2, ET):
                    j, r = t - 2, (u - 2) % 2
                    ex = expert_of[2]
                    pe.wait_ge(s_elo, j + 1)
                    if known is None or known - 2 >= 2:
                        pe.wait_ge(s_ey, j - 1)
                    for s in range(2):
                        n = 0
                        for xp, wp in PARTS:
                            for kt in range(KT):
                                w = w12[:, bass.ds(ex, 1), 1, wp, kt, :].rearrange("p o n -> p (o n)")
                                last = mm(fold[r][:, s * H:s * H + H], ehl[:, r, xp, kt, s * P:s * P + P], w,
                                          start=(n == 0), stop=(n == 3 * KT - 1))
                                n += 1
                    last.then_inc(s_eyp, 1)

            pe.wait_ge(s_tab, 2)
            pe.wait_ge(s_el, 2 * E)
            run(pe, expert_step, ((1, 5),), ET + 2, 2 * B)


_INS = ['x', 'adj', 'L0_gnn_W_self', 'L0_gnn_b_self', 'L0_gnn_W_nb', 'L0_gnn_b_nb', 'L0_gnn_W_comb', 'L0_gnn_b_comb',
        'L0_ffn_Wg', 'L0_ffn_bg', 'L0_ffn_W1', 'L0_ffn_b1', 'L0_ffn_W2', 'L0_ffn_b2']


def kernel(**inputs):
    import numpy as _np
    import concourse.bacc as _bacc
    from concourse import mybir as _mybir
    from concourse.bass_utils import run_bass_kernel_spmd as _run

    nc = _bacc.Bacc("TRN2", target_bir_lowering=False, num_devices=1)
    arrays, args = {}, []
    for name in _INS:
        a = _np.ascontiguousarray(inputs[name])
        arrays[f"in_{name}_dram"] = a
        args.append(nc.dram_tensor(f"in_{name}_dram", a.shape, _mybir.dt.from_np(a.dtype), kind="ExternalInput").ap())
    args.append(nc.dram_tensor("out_0_dram", inputs['x'].shape, _mybir.dt.float32, kind="ExternalOutput").ap())
    gnn_moe_kernel(nc, *args)
    r = _run(nc, [arrays], core_ids=[0])
    return r.results[0]["out_0_dram"]
```
